# Optimizing a Trainium2 kernel written in Bass

```python
import numpy as np
import jax
import jax.numpy as jnp

def _softmax(x, axis=-1):
    return jax.nn.softmax(x, axis=axis)

def _gelu(x):
    return jax.nn.gelu(x, approximate=True)

def _silu(x):
    return jax.nn.silu(x)

def _sigmoid(x):
    return jax.nn.sigmoid(x)

def _layernorm(x, axis=-1, eps=1e-05):
    m = jnp.mean(x, axis=axis, keepdims=True)
    v = jnp.var(x, axis=axis, keepdims=True)
    return (x - m) / jnp.sqrt(v + eps)

def _scatter_add(tgt, idx, src, axis=0):
    return tgt.at[idx].add(src)

def _segment_sum(src, seg, n):
    return jax.ops.segment_sum(src, seg, n)
kernel_name = 'mk_flamingo_gated_d2_seqx_r8_51e04c'

def setup_inputs(seed: int=0):
    np.random.seed(seed)
    _w = jnp.asarray

    def _rec_inputs():
        import jax
        import jax.numpy as jnp
        _rk = jax.random.key(seed)
        x = -0.0003929 + 0.9999 * jax.random.normal(jax.random.fold_in(_rk, 1), (4, 256, 512), jnp.float32)
        _lenS = 256 - jax.random.randint(jax.random.fold_in(_rk, 7), (4,), 0, max(1, 256 // 4) + 1, jnp.int32)
        _lenS2 = 1601 - jax.random.randint(jax.random.fold_in(_rk, 8), (4,), 0, max(1, 1601 // 4) + 1, jnp.int32)
        _ctx_4096P = jax.random.normal(jax.random.fold_in(_rk, 11), (4, 16, 512), jnp.float32)
        _ctx_4096c = jax.random.dirichlet(jax.random.fold_in(_rk, 511), 0.3 * jnp.ones((16,), jnp.float32), (4, 1601))
        _ctx_4096t = jnp.einsum('bsk,bkd->bsd', _ctx_4096c, _ctx_4096P)
        _ctx_4096t = _ctx_4096t * jax.lax.rsqrt(jnp.mean(jnp.square(_ctx_4096t)) + 1e-12) * 0.953939
        ctx_4096 = 2.81802e-05 + 1.00001 * (_ctx_4096t + 0.3 * jax.random.normal(jax.random.fold_in(_rk, 611), (4, 1601, 512), jnp.float32))
        _validS = jnp.arange(256)[None, :] < _lenS[:, None]
        _validS2 = jnp.arange(1601)[None, :] < _lenS2[:, None]
        _causal = jnp.tril(jnp.ones((256, 256), dtype=bool))
        mask_SxS2_bk0 = jnp.logical_not(jnp.broadcast_to(_validS2[0:1, :], (256, 1601)))
        _g = jax.random.normal(jax.random.fold_in(_rk, 9001), (2, 2), jnp.float32)
        _g = jnp.sign(_g) * jnp.maximum(jnp.abs(_g), 1.0) + (_g == 0) * 1.0
        g_xattn = _g[0]
        g_ffn = _g[1]
        return (x, ctx_4096, mask_SxS2_bk0, g_xattn, g_ffn)
    x, ctx_4096, mask_SxS2_bk0, g_xattn, g_ffn = _rec_inputs()

    def _L0_xattn_setup():
        import jax, jax.numpy as jnp
        import numpy as np
        N_HEAD = 32
        D_MODEL = 512
        N_KV_GROUPS = 8
        D_HEAD = D_MODEL // N_HEAD
        H_PER_G = N_HEAD // N_KV_GROUPS
        KV_DIM = N_KV_GROUPS * D_HEAD
        B, S = (2, 256)
        key = jax.random.key(seed)
        ks = jax.random.split(key, 8)
        q = jax.random.normal(ks[0], (B, S, D_MODEL), dtype=jnp.float32)
        k = jax.random.normal(ks[1], (B, S, D_MODEL), dtype=jnp.float32)
        v = jax.random.normal(ks[2], (B, S, D_MODEL), dtype=jnp.float32)
        mask = jnp.tril(jnp.ones((S, S), dtype=bool))
        w_q = jax.random.uniform(ks[3], (D_MODEL, D_MODEL), dtype=jnp.float32) * 0.02
        w_k = jax.random.uniform(ks[4], (KV_DIM, D_MODEL), dtype=jnp.float32) * 0.02
        w_v = jax.random.uniform(ks[5], (KV_DIM, D_MODEL), dtype=jnp.float32) * 0.02
        w_out = jax.random.uniform(ks[6], (D_MODEL, D_MODEL), dtype=jnp.float32) * 0.02
        return {'q': q, 'k': k, 'v': v, 'w_q': w_q, 'w_k': w_k, 'w_v': w_v, 'w_out': w_out, 'mask': mask}
    _L0_xattn_all = _L0_xattn_setup()
    _L0_xattn_in = {k: v for k, v in _L0_xattn_all.items() if k in ('w_q', 'w_k', 'w_v', 'w_out')}
    del _L0_xattn_all

    def _L0_ffn_setup():
        import jax, jax.numpy as jnp
        import numpy as np
        B, T, D_IN, D_OUT = (8, 256, 512, 512)
        N_LORAS, RANK = (16, 32)
        SCALING = 1.0
        key = jax.random.key(seed)
        ks = jax.random.split(key, 8)
        std = 1.0 / D_IN ** 0.5
        x = jax.random.normal(ks[0], (B, T, D_IN), dtype=jnp.float32)
        idx = jax.random.randint(ks[1], (B,), 0, N_LORAS)
        gate = jax.nn.one_hot(idx, N_LORAS, dtype=jnp.float32)
        kernel = jax.random.normal(ks[2], (D_IN, D_OUT), dtype=jnp.float32) * std
        bias = jnp.zeros((D_OUT,), dtype=jnp.float32)
        lora_A = jax.random.normal(ks[3], (N_LORAS, RANK, D_IN), dtype=jnp.float32) * std
        lora_B = jax.random.normal(ks[4], (N_LORAS, D_OUT, RANK), dtype=jnp.float32) * 0.01
        lora_A_shared = jax.random.normal(ks[5], (RANK, D_IN), dtype=jnp.float32) * std
        lora_B_shared = jax.random.normal(ks[6], (D_OUT, RANK), dtype=jnp.float32) * 0.01
        return {'x': x, 'gate': gate, 'kernel': kernel, 'bias': bias, 'lora_A': lora_A, 'lora_B': lora_B, 'lora_A_shared': lora_A_shared, 'lora_B_shared': lora_B_shared}
    _L0_ffn_all = _L0_ffn_setup()
    _L0_ffn_in = {k: v for k, v in _L0_ffn_all.items() if k in ('gate', 'kernel', 'bias', 'lora_A', 'lora_B', 'lora_A_shared', 'lora_B_shared')}
    del _L0_ffn_all

    def _L1_xattn_setup():
        import jax, jax.numpy as jnp
        import numpy as np
        B, Q, D = (8, 64, 512)
        CTX = 512
        H, KV, HD = (16, 4, 96)
        G = H // KV
        key = jax.random.key(seed)
        ks = jax.random.split(key, 6)
        s = 0.02
        return {'latents': jax.random.normal(ks[0], (B, Q, D), jnp.float32), 'context': jax.random.normal(ks[1], (B, CTX, D), jnp.float32), 'Wq': jax.random.normal(ks[2], (H * HD, D), jnp.float32) * s, 'Wk': jax.random.normal(ks[3], (KV * HD, D), jnp.float32) * s, 'Wv': jax.random.normal(ks[4], (KV * HD, D), jnp.float32) * s, 'Wo': jax.random.normal(ks[5], (D, H * HD), jnp.float32) * s}
    _L1_xattn_all = _L1_xattn_setup()
    _L1_xattn_in = {k: v for k, v in _L1_xattn_all.items() if k in ('Wq', 'Wk', 'Wv', 'Wo')}
    del _L1_xattn_all

    def _L1_ffn_setup():
        import jax, jax.numpy as jnp
        import numpy as np
        R = 16
        LORA_ALPHA = 16
        SCALING = LORA_ALPHA / R
        key = jax.random.key(seed)
        kx, kr, ka = jax.random.split(key, 3)
        B, S, D, DO, E = (4, 256, 512, 512, 8)
        x = jax.random.normal(kx, (B, S, D), dtype=jnp.float32)
        bound_r = 1.0 / np.sqrt(D)
        route_w = jax.random.uniform(kr, (E, D), jnp.float32, -bound_r, bound_r)
        bound_a = 1.0 / np.sqrt(D)
        A = jax.random.uniform(ka, (E, R, D), jnp.float32, -bound_a, bound_a)
        kb = jax.random.fold_in(key, 7)
        Bw = jax.random.normal(kb, (E, DO, R), dtype=jnp.float32) * 0.02
        return {'x': x, 'route_w': route_w, 'A': A, 'Bw': Bw}
    _L1_ffn_all = _L1_ffn_setup()
    _L1_ffn_in = {k: v for k, v in _L1_ffn_all.items() if k in ('route_w', 'A', 'Bw')}
    del _L1_ffn_all
    return {'x': x, 'ctx_4096': ctx_4096, 'mask_SxS2_bk0': mask_SxS2_bk0, 'g_xattn': g_xattn, 'g_ffn': g_ffn, 'L0_xattn_w_q': _L0_xattn_in['w_q'], 'L0_xattn_w_k': _L0_xattn_in['w_k'], 'L0_xattn_w_v': _L0_xattn_in['w_v'], 'L0_xattn_w_out': _L0_xattn_in['w_out'], 'L0_ffn_gate': _L0_ffn_in['gate'], 'L0_ffn_kernel': _L0_ffn_in['kernel'], 'L0_ffn_bias': _L0_ffn_in['bias'], 'L0_ffn_lora_A': _L0_ffn_in['lora_A'], 'L0_ffn_lora_B': _L0_ffn_in['lora_B'], 'L0_ffn_lora_A_shared': _L0_ffn_in['lora_A_shared'], 'L0_ffn_lora_B_shared': _L0_ffn_in['lora_B_shared'], 'L1_xattn_Wq': _L1_xattn_in['Wq'], 'L1_xattn_Wk': _L1_xattn_in['Wk'], 'L1_xattn_Wv': _L1_xattn_in['Wv'], 'L1_xattn_Wo': _L1_xattn_in['Wo'], 'L1_ffn_route_w': _L1_ffn_in['route_w'], 'L1_ffn_A': _L1_ffn_in['A'], 'L1_ffn_Bw': _L1_ffn_in['Bw']}

def reference(x, ctx_4096, mask_SxS2_bk0, g_xattn, g_ffn, L0_xattn_w_q, L0_xattn_w_k, L0_xattn_w_v, L0_xattn_w_out, L0_ffn_gate, L0_ffn_kernel, L0_ffn_bias, L0_ffn_lora_A, L0_ffn_lora_B, L0_ffn_lora_A_shared, L0_ffn_lora_B_shared, L1_xattn_Wq, L1_xattn_Wk, L1_xattn_Wv, L1_xattn_Wo, L1_ffn_route_w, L1_ffn_A, L1_ffn_Bw):
    import jax
    import jax.numpy as jnp

    def _L0_xattn_ref(q, k, v, w_q, w_k, w_v, w_out, mask):
        import jax, jax.numpy as jnp
        import numpy as np
        N_HEAD = 32
        D_MODEL = 512
        N_KV_GROUPS = 8
        D_HEAD = D_MODEL // N_HEAD
        H_PER_G = N_HEAD // N_KV_GROUPS
        KV_DIM = N_KV_GROUPS * D_HEAD
        B, S = (2, 256)
        b, n, _ = q.shape
        s = k.shape[1]
        query = q @ w_q.T
        key = k @ w_k.T
        value = v @ w_v.T
        query = query.reshape(b, n, N_HEAD, D_HEAD).transpose(0, 2, 1, 3)
        query = query.reshape(b, N_KV_GROUPS, H_PER_G, n, D_HEAD)
        key = key.reshape(b, s, N_KV_GROUPS, D_HEAD).transpose(0, 2, 1, 3)
        value = value.reshape(b, s, N_KV_GROUPS, D_HEAD).transpose(0, 2, 1, 3)
        scores = jnp.einsum('bghnd,bgsd->bghns', query, key) / D_HEAD ** 0.5
        scores = jnp.where(mask, scores, jnp.finfo(scores.dtype).min)
        attention = jax.nn.softmax(scores, axis=-1)
        out = jnp.einsum('bghns,bgsd->bghnd', attention, value)
        out = out.transpose(0, 3, 1, 2, 4).reshape(b, n, D_MODEL)
        return out @ w_out.T

    def _L0_ffn_ref(x, gate, kernel, bias, lora_A, lora_B, lora_A_shared, lora_B_shared):
        import jax, jax.numpy as jnp
        import numpy as np
        B, T, D_IN, D_OUT = (8, 256, 512, 512)
        N_LORAS, RANK = (16, 32)
        SCALING = 1.0
        base_out = jnp.matmul(x, kernel) + bias
        b = gate.shape[0]
        x_flat = x.reshape(b, -1, x.shape[-1])
        A_eff = jnp.einsum('bn,nri->bri', gate, lora_A)
        B_eff = jnp.einsum('bn,nor->bor', gate, lora_B)
        Ax = jnp.einsum('bri,bti->btr', A_eff, x_flat)
        delta_flat = jnp.einsum('bor,btr->bto', B_eff, Ax)
        Ax_s = jnp.einsum('ri,bti->btr', lora_A_shared, x_flat)
        delta_flat = delta_flat + jnp.einsum('or,btr->bto', lora_B_shared, Ax_s)
        delta = delta_flat.reshape(x.shape[:-1] + (kernel.shape[-1],))
        return base_out + (SCALING * delta).astype(base_out.dtype)

    def _L1_xattn_ref(latents, context, Wq, Wk, Wv, Wo):
        import jax, jax.numpy as jnp
        import numpy as np
        B, Q, D = (8, 64, 512)
        CTX = 512
        H, KV, HD = (16, 4, 96)
        G = H // KV
        b, q_len, _ = latents.shape
        hidden = jnp.concatenate([context, latents], axis=1)
        s_len = hidden.shape[1]
        q = (latents @ Wq.T).reshape(b, q_len, H, HD)
        k = (hidden @ Wk.T).reshape(b, s_len, KV, HD)
        v = (hidden @ Wv.T).reshape(b, s_len, KV, HD)
        q = q.transpose(0, 2, 1, 3).reshape(b, KV, G, q_len, HD)
        k = k.transpose(0, 2, 1, 3)
        v = v.transpose(0, 2, 1, 3)
        scale = 1.0 / jnp.sqrt(jnp.asarray(HD, q.dtype))
        scores = jnp.einsum('bkgqd,bksd->bkgqs', q, k) * scale
        attn = jax.nn.softmax(scores.astype(jnp.float32), axis=-1).astype(q.dtype)
        out = jnp.einsum('bkgqs,bksd->bkgqd', attn, v)
        out = out.reshape(b, H, q_len, HD).transpose(0, 2, 1, 3).reshape(b, q_len, H * HD)
        return out @ Wo.T

    def _L1_ffn_ref(x, route_w, A, Bw):
        import jax, jax.numpy as jnp
        import numpy as np
        R = 16
        LORA_ALPHA = 16
        SCALING = LORA_ALPHA / R
        logits = jnp.einsum('bsd,ed->bse', x, route_w)
        topk_v, topk_idx = jax.lax.top_k(logits, 1)
        E = logits.shape[-1]
        route_weight = jax.nn.one_hot(topk_idx[..., 0], E, dtype=logits.dtype) * topk_v
        h = jnp.einsum('bsd,erd->bser', x, A)
        wh = route_weight[..., None] * h
        out = jnp.einsum('bser,eor->bso', wh, Bw) * SCALING
        return out
    x = x + jnp.tanh(g_xattn[0]) * _L0_xattn_ref(_layernorm(x, axis=-1), ctx_4096, ctx_4096, L0_xattn_w_q, L0_xattn_w_k, L0_xattn_w_v, L0_xattn_w_out, mask_SxS2_bk0)
    x = x + jnp.tanh(g_ffn[0]) * _L0_ffn_ref(_layernorm(x, axis=-1), L0_ffn_gate, L0_ffn_kernel, L0_ffn_bias, L0_ffn_lora_A, L0_ffn_lora_B, L0_ffn_lora_A_shared, L0_ffn_lora_B_shared)
    x = x + jnp.tanh(g_xattn[1]) * _L1_xattn_ref(_layernorm(x, axis=-1), ctx_4096, L1_xattn_Wq, L1_xattn_Wk, L1_xattn_Wv, L1_xattn_Wo)
    x = x + jnp.tanh(g_ffn[1]) * _L1_ffn_ref(_layernorm(x, axis=-1), L1_ffn_route_w, L1_ffn_A, L1_ffn_Bw)
    return x

_drawn_inputs = setup_inputs


def setup_inputs(seed=0):
    import zlib

    import numpy as np

    out = dict(_drawn_inputs(seed))
    spreads = {'g_ffn': (-1.0, 0.6), 'L0_ffn_bias': (0.0, 0.1)}
    factors = {'L0_xattn_w_q': 8.0,
     'L0_xattn_w_k': 8.0,
     'L0_xattn_w_out': 4.565,
     'L1_xattn_Wq': 6.724,
     'L1_xattn_Wk': 6.466}
    for name, (base, spread) in spreads.items():
        noise = np.random.default_rng([zlib.crc32(name.encode()), seed]).standard_normal(out[name].shape)
        drawn = base * np.exp(spread * noise) if base else spread * noise
        out[name] = jnp.asarray(drawn.astype(out[name].dtype))
    for name, factor in factors.items():
        out[name] = (out[name] * factor).astype(out[name].dtype)
    return out
```

```python
from contextlib import ExitStack

import concourse.bass as bass
from concourse import mybir

ALU = mybir.AluOpType
ACT = mybir.ActivationFunctionType
AX = mybir.AxisListType
F32 = mybir.dt.float32
F32R = mybir.dt.float32r
BF16 = mybir.dt.bfloat16
U8 = mybir.dt.uint8

P = 128
BANK = 512
MASKED = -3.3895313892515355e38
EPS = 1e-5


def pieces(total, n):
    base, extra = divmod(total, n)
    out, at = [], 0
    for i in range(n):
        w = base + (i < extra)
        out.append((at, w))
        at += w
    return out


def flamingo_kernel(nc, x, ctxT, mask, maskT, g_xattn, g_ffn, wq0, wk0, wv0, wo0, gate_rep, dense,
                    bias, loraA, loraB, sharedA, sharedB, wq1, wk1, wv1, wo1, routeT, expertA,
                    expertB, out, phases="AB"):
    B, D, N0 = ctxT.shape
    Q = x.shape[0] // B
    QT = Q // P
    KC = D // P
    TILES = B * QT
    G0, J, D0 = 8, 4, 16
    HQ = J * Q
    PART_Q, PART_K = (0, 1, 2, 0, 1, 0), (0, 0, 0, 1, 1, 2)
    R0 = len(PART_Q) * D0
    KT0 = [(s, min(P, N0 - s)) for s in range(0, N0, P)]
    CH0 = pieces(N0, 4)
    NC0 = len(CH0)
    RANK, NL = 32, 16
    G1, D1 = 4, 96
    N1 = Q + N0
    KT1 = [(s, P) for s in range(0, Q, P)] + [(Q + s, w) for s, w in KT0]
    CW1 = -(-N1 // 4) + (-(-N1 // 4)) % 2
    CH1 = [(min(i * CW1, N1 - CW1), CW1) for i in range(4)]
    E1, RK1 = 8, 16
    ROWS = J * QT
    NS = ROWS * NC0

    with ExitStack() as ctx:
        def sb(name, shape, dt, to=ctx):
            return to.enter_context(nc.sbuf_tensor(name, shape, dt))

        def sem(name):
            return ctx.enter_context(nc.semaphore(name))

        PS = ctx.enter_context(nc.psum_tensor("PS", [P, 8, BANK], F32))

        X = sb("X", [P, TILES * D], F32)
        C = sb("C", [P, KC, N0], F32)
        ident = sb("ident", [P, P], F32)
        gates = sb("gates", [P, 4], F32)
        tg = sb("tg", [P, 4], F32)
        stats = sb("stats", [P, QT, 6], F32)
        mv = sb("mv", [P, QT, 2], F32)
        vpe = sb("vpe", [P, QT], F32)
        std = sb("std", [P, QT], F32)
        rstd = sb("rstd", [P, QT], F32)
        XN = sb("XN", [P, QT, D], F32)
        XNT = sb("XNT", [P, KC, Q], F32)
        PT = sb("PT", [P, 2, HQ], F32)
        pm = sb("pm", [P, ROWS, NC0], F32)
        nm = sb("nm", [P, ROWS], F32)

        KD = nc.dram_tensor("KD", (3, P, N0), BF16).ap()
        QD = nc.dram_tensor("QD", (3, P, HQ), BF16).ap()

        mA = ExitStack()
        identb = sb("identb", [P, P], BF16, mA)
        selA = sb("selA", [P, P], F32, mA)
        eye32 = sb("eye32", [P, 4, RANK], F32, mA)
        onesr = sb("onesr", [1, P], F32, mA)
        Wq = sb("Wq", [P, KC, D], F32, mA)
        Wk = sb("Wk", [P, KC, P], F32, mA)
        Wv = sb("Wv", [P, KC, P], F32, mA)
        WoX = sb("WoX", [P, G0, D], F32, mA)
        Wd = sb("Wd", [P, KC, D], F32, mA)
        LA = sb("LA", [P, KC, NL * RANK], F32, mA)
        LB = sb("LB", [P, 4, D], F32, mA)
        SA = sb("SA", [P, KC, RANK], F32, mA)
        SB = sb("SB", [RANK, D], F32, mA)
        biasr = sb("biasr", [1, D], F32, mA)
        gcol = sb("gcol", [P, TILES * 4], F32, mA)
        bytes8 = PT[:].rearrange("p a n -> p (a n)").bitcast(U8)
        m8 = bytes8[:, 0:QT * N0].rearrange("p (t n) -> p t n", n=N0)
        mT8 = bytes8[:, QT * N0:QT * N0 + len(KT0) * Q].rearrange("p (t q) -> p t q", q=Q)
        mq = sb("mq", [P, QT, N0], BF16, mA)
        mT = sb("mT", [P, len(KT0), Q], BF16, mA)
        KS = sb("KS", [P, 3, N0 + N0 % 2], BF16, mA)
        QS = sb("QS", [P, 3, HQ], BF16, mA)
        RS = sb("RS", [P, 2, BANK], F32, mA)
        KX = sb("KX", [R0 + 2, G0, N0], BF16, mA)
        QX = sb("QX", [R0 + 2, G0, HQ], BF16, mA)
        VX = sb("VX", [P, len(KT0), G0, 2 * D0], F32, mA)
        NMT = sb("NMT", [ROWS, 2, P], BF16, mA)
        OS = sb("OS", [P, 2, Q], F32, mA)
        RC = sb("RC", [P, Q], F32, mA)
        AXS = sb("AXS", [RANK, Q], F32, mA)
        junk = RS[:].bitcast(BF16)
        ON = KS[:].rearrange("p a n -> p (a n)")[:, 0:2 * G0 * Q].bitcast(F32).rearrange("p (g q) -> p g q", q=Q)
        RP = QS[:].rearrange("p a n -> p (a n)")[:, 0:2 * QT * 4 * P].bitcast(F32).rearrange("p (i k) -> p i k", k=P)
        AXA = PT[:, 0, :].rearrange("p (c q) -> p c q", q=Q)
        GA = PT[:, 1, :].rearrange("p (t c q) -> p t c q", t=QT, c=4)
        mA.close()

        mB = ExitStack()
        sel1 = sb("sel1", [D1 + 1, D1], F32, mB)
        Wk1 = sb("Wk1", [P, KC, G1 * D1], F32, mB)
        Wv1 = sb("Wv1", [P, KC, G1 * D1], F32, mB)
        Wq1 = sb("Wq1", [P, KC, G1 * J * D1], F32, mB)
        Wo1 = sb("Wo1", [D1, 2, J, D], F32, mB)
        WR = sb("WR", [P, KC, P + E1], F32, mB)
        WB = sb("WB", [P, D], F32, mB)
        K1H = sb("K1H", [D1 + 2, 2, N1], F32R, mB)
        K1L = sb("K1L", [D1, 2, N1], F32R, mB)
        Q1H = sb("Q1H", [D1 + 2, 2, HQ], F32R, mB)
        Q1L = sb("Q1L", [D1, 2, HQ], F32R, mB)
        V1 = sb("V1", [P, len(KT1), G1, D1 + 1], F32, mB)
        NMT1 = sb("NMT1", [ROWS, 2, P], F32R, mB)
        OS1 = sb("OS1", [D1 + 1, HQ], F32, mB)
        RC1 = sb("RC1", [D1, HQ], F32, mB)
        ON1 = sb("ON1", [D1, HQ], F32, mB)
        top = sb("top", [P, QT, 4], F32, mB)
        lgt = sb("lgt", [P, QT, 4, E1], F32, mB)
        rank = sb("rank", [P, E1], F32, mB)
        WH = sb("WH", [P, QT, P], F32, mB)
        WHT = sb("WHT", [P, Q], F32, mB)
        mB.close()

        spent = sem("spent")
        consts = sem("consts")
        loaded_x = sem("loaded_x")
        loaded_kv = sem("loaded_kv")
        loaded_q = sem("loaded_q")
        loaded_mask = sem("loaded_mask")
        loaded_gates = sem("loaded_gates")
        loaded_rest = sem("loaded_rest")
        masks_made = sem("masks_made")
        tanh_done = sem("tanh_done")
        ctx_loaded = sem("ctx_loaded")
        ln_step = sem("ln_step")
        var_ready = sem("var_ready")
        std_ready = sem("std_ready")
        xn_ready = sem("xn_ready")
        xnt_ready = sem("xnt_ready")
        xnt_copied = sem("xnt_copied")
        prod_ready = sem("prod_ready")
        hi_done = sem("hi_done")
        rest_done = sem("rest_done")
        mid_done = sem("mid_done")
        lo_done = sem("lo_done")
        v_ready = sem("v_ready")
        v_copied = sem("v_copied")
        k_parked = sem("k_parked")
        k_stacked = sem("k_stacked")
        q_parked = sem("q_parked")
        q_stacked = sem("q_stacked")
        s_ready = sem("s_ready")
        max_done = sem("max_done")
        nm_ready = sem("nm_ready")
        nmt_ready = sem("nmt_ready")
        nmt_split = sem("nmt_split")
        m_rows = sem("m_rows")
        st_ready = sem("st_ready")
        exp_done = sem("exp_done")
        pv_done = sem("pv_done")
        o_copied = sem("o_copied")
        den_ready = sem("den_ready")
        rec_done = sem("rec_done")
        on_ready = sem("on_ready")
        y_ready = sem("y_ready")
        x_done = sem("x_done")
        rp_ready = sem("rp_ready")
        ax_ready = sem("ax_ready")
        ax_copied = sem("ax_copied")
        rep_ready = sem("rep_ready")
        ga_ready = sem("ga_ready")
        loaded_b1 = sem("loaded_b1")
        loaded_b2 = sem("loaded_b2")
        consts_b = sem("consts_b")
        wo_loaded = [sem("wo_loaded_0"), sem("wo_loaded_1")]
        v1_ready = sem("v1_ready")
        v1_copied = sem("v1_copied")
        item_ready = sem("item_ready")
        item_hi = sem("item_hi")
        item_done = sem("item_done")
        st1_ready = sem("st1_ready")
        exp1_done = sem("exp1_done")
        pv1_done = sem("pv1_done")
        o1_copied = sem("o1_copied")
        rec1_done = sem("rec1_done")
        h_ready = sem("h_ready")
        rt_step = sem("rt_step")
        wh_ready = sem("wh_ready")
        wht_ready = sem("wht_ready")
        wht_copied = sem("wht_copied")
        stored = sem("stored")

        def xt(b, qt):
            return X[:, bass.ds(b * (QT * D) + qt * D, D)]

        def after(b, per, k, base=0):
            return b * per + (base + k)

        XB = 4 * B + 1

        def apart(eng):
            eng.sem_inc(spent, 1)

        block = ctx.enter_context(nc.Block())

        def group_items(g):
            return ([("K", g, c) for c in range(1 + NC0)] + [("Q", g, c) for c in range(2)]
                    + [("S", g, i) for i in range(NS)] + [("M", g, 0)])

        def finish_items(g):
            return [("D", g, h) for h in range(2)] + [("Y", g, qt) for qt in range(QT)]

        items = group_items(0)
        window_end = []
        for g in range(G1):
            if g >= 1:
                items += finish_items(g - 1)
            if g + 1 < G1:
                items += group_items(g + 1)
            window_end.append(len(items))
        items += finish_items(G1 - 1)
        NI = len(items)
        assert NI % 2 == 0
        where = {it: n for n, it in enumerate(items)}
        NHI = sum(it[0] in "KQ" for it in items)
        hi_order = {it: n for n, it in enumerate([it for it in items if it[0] in "KQ"])}
        NP1 = len(KT1) * G1
        assert NP1 % 2 == 0 and (len(KT0) * G0) % 2 == 0

        def step_items(g, t):
            start = where[("M", 0, 0)] + 1 if g == 0 else window_end[g - 1]
            end = window_end[g]

            def upto(t):
                if t < 0 or (t == 0 and g >= 1):
                    return start
                return min(start + -(-(end - start) * (t + 1) // (len(KT1) - 2)), end)
            return upto(t - 1), upto(t)

        def split_part(n, part):
            if n < 4:
                s, w = CH0[n]
                return KS[:, part, s:s + w]
            return QS[:, part, (n - 4) * BANK:(n - 3) * BANK]

        def half_of(n, k_tile, q_tile):
            kind, g, i = items[n]
            if kind == "K":
                s, w = (0, Q) if i == 0 else (Q + CH0[i - 1][0], CH0[i - 1][1])
                return k_tile[0:D1, g % 2, s:s + w], w
            return q_tile[0:D1, g % 2, i * BANK:(i + 1) * BANK], BANK

        def copy_out(b, g):
            ae = nc.scalar
            ae.wait_ge(pv_done, after(b, G0 * len(KT0), (g + 1) * len(KT0)))
            if g >= 2:
                ae.wait_ge(on_ready, after(b, G0, g - 1))
            ae.copy(OS[:, g % 2, :], PS[:, 6 + g % 2, 0:Q]).then_inc(o_copied, 1)

        def copy_out1(b, g):
            ae = nc.scalar
            ae.wait_ge(pv1_done, after(b, NP1, (g + 1) * len(KT1)))
            if g >= 1:
                ae.wait_ge(item_done, after(b, NI, where[("D", g - 1, 1)] + 1))
            ae.copy(OS1[:], PS[0:D1 + 1, 6:8, :].rearrange("p a n -> p (a n)")).then_inc(o1_copied, 1)

        @block.sync
        def _(sp):
            sp.dma_start(X[:].rearrange("p (t d) -> p t d", d=D),
                         x.rearrange("(t p) d -> p t d", p=P)).then_inc(loaded_x, 16)
            sp.dma_start(Wk[:], wk0.rearrange("(c p) n -> p c n", p=P)).then_inc(loaded_kv, 16)
            sp.dma_start(Wv[:], wv0.rearrange("(c p) n -> p c n", p=P)).then_inc(loaded_kv, 16)
            sp.dma_start(Wq[:], wq0.rearrange("(c p) n -> p c n", p=P)).then_inc(loaded_q, 16)
            sp.dma_start(m8, mask.rearrange("(t p) n -> p t n", p=P)).then_inc(loaded_mask, 16)
            full = N0 // P
            sp.dma_start(mT8[:, 0:full, :], maskT[0:full * P, :].rearrange("(t p) q -> p t q", p=P)
                         ).then_inc(loaded_mask, 16)
            sp.dma_start(mT8[0:N0 - full * P, full, :], maskT[full * P:N0, :]).then_inc(loaded_mask, 16)
            sp.dma_start(gates[:, 0:2], g_xattn.partition_broadcast(P)).then_inc(loaded_gates, 16)
            sp.dma_start(gates[:, 2:4], g_ffn.partition_broadcast(P)).then_inc(loaded_gates, 16)
            sp.wait_ge(consts, 5)
            for j in range(J):
                sp.dma_start(WoX[32 * j:32 * j + D0, :, :],
                             wo0.rearrange("(g j d) n -> j d g n", g=G0, j=J)[j]).then_inc(loaded_rest, 16)
            for dst, src in ((Wd, dense), (LA, loraA), (SA, sharedA)):
                sp.dma_start(dst[:], src.rearrange("(c p) n -> p c n", p=P)).then_inc(loaded_rest, 16)
            sp.dma_start(LB[:], loraB.rearrange("(c p) n -> p c n", p=P)).then_inc(loaded_rest, 16)
            sp.dma_start(SB[:], sharedB).then_inc(loaded_rest, 16)
            sp.dma_start(biasr[:], bias).then_inc(loaded_rest, 16)
            sp.dma_start(gcol[:], gate_rep).then_inc(loaded_rest, 16)

            with sp.Fori(0, B) as b:
                sp.wait_ge(x_done, after(b, 4, 0, 1))
                sp.wait_ge(lo_done, after(b, 6, 4))
                sp.dma_start(KD.rearrange("a p n -> p a n"), KS[:, :, 0:N0]).then_inc(k_parked, 16)
                sp.wait_ge(k_parked, after(b, 16, 16))
                for r, part in enumerate(PART_K):
                    sp.dma_start(KX[D0 * r:D0 * r + D0, :, :], KD[part].rearrange("(g d) n -> d g n", g=G0)
                                 ).then_inc(k_stacked, 16)
                sp.wait_ge(lo_done, after(b, 6, 6))
                sp.dma_start(QD.rearrange("a p n -> p a n"), QS[:]).then_inc(q_parked, 16)
                sp.wait_ge(q_parked, after(b, 16, 16))
                for r, part in enumerate(PART_Q):
                    sp.dma_start(QX[D0 * r:D0 * r + D0, :, :], QD[part].rearrange("(g d) n -> d g n", g=G0)
                                 ).then_inc(q_stacked, 16)
                for g in range(G0):
                    sp.wait_ge(nmt_split, after(b, 2 * G0, 2 * g + 2))
                    for s in range(2):
                        sp.dma_start(QX[R0 + s:R0 + s + 1, g, :].rearrange("o (c q) -> o c q", q=P),
                                     NMT[:, s, :]).then_inc(m_rows, 16)

            if "B" in phases:
                sp.wait_ge(x_done, XB)
                sp.dma_start(Wk1[:], wk1.rearrange("(c p) n -> p c n", p=P)).then_inc(loaded_b1, 16)
                sp.dma_start(Wv1[:], wv1.rearrange("(c p) n -> p c n", p=P)).then_inc(loaded_b1, 16)
                sp.dma_start(Wq1[:], wq1.rearrange("(c p) n -> p c n", p=P)).then_inc(loaded_b1, 16)
                sp.dma_start(WR[:, :, 0:P], expertA.rearrange("(c p) n -> p c n", p=P)).then_inc(loaded_b2, 16)
                sp.dma_start(WR[:, :, P:P + E1], routeT.rearrange("(c p) n -> p c n", p=P)).then_inc(loaded_b2, 16)
                sp.dma_start(WB[:], expertB).then_inc(loaded_b2, 16)
                with sp.Fori(0, B) as b:
                    for g in range(G1):
                        sp.wait_ge(nmt_split, after(b, 2 * G1, 2 * g + 2, 2 * G0 * B))
                        for s in range(2):
                            sp.dma_start(Q1H[D1 + s:D1 + s + 1, g % 2, :].bitcast(F32).rearrange("o (c q) -> o c q", q=P),
                                         NMT1[:, s, :].bitcast(F32)).then_inc(m_rows, 16)
                    for qt in range(QT):
                        sp.wait_ge(x_done, after(b, 2, qt + 1, XB))
                        sp.dma_start(out[bass.ds(b * Q + qt * P, P), :], xt(b, qt)).then_inc(stored, 16)
                sp.wait_ge(stored, 16 * QT * B)
            else:
                sp.wait_ge(x_done, XB)
                sp.dma_start(out.rearrange("(t p) d -> p t d", p=P),
                             X[:].rearrange("p (t d) -> p t d", d=D)).then_inc(stored, 16)
                sp.wait_ge(stored, 16)

        @block.gpsimd
        def _(pool):
            def eye(tile, pattern, base, n):
                pool.wait_ge(consts, n)
                return nc.gpsimd.affine_select(out=tile, in_=tile, compare_op=ALU.not_equal, fill=1.0,
                                               base=base, pattern=pattern, channel_multiplier=1)

            nc.gpsimd.memset(ident[:], 0.0).then_inc(consts, 1)
            nc.gpsimd.memset(identb[:], 0.0).then_inc(consts, 1)
            nc.gpsimd.memset(selA[:], 0.0).then_inc(consts, 1)
            nc.gpsimd.memset(eye32[:], 0.0).then_inc(consts, 1)
            nc.gpsimd.memset(WoX[:], 0.0).then_inc(consts, 1)
            nc.gpsimd.memset(VX[:, :, :, D0:2 * D0], 1.0).then_inc(consts, 1)
            pool.wait_ge(consts, 6)
            nc.gpsimd.memset(KX[R0:R0 + 2, :, :], 1.0).then_inc(consts, 1)
            pool.wait_ge(consts, 7)
            nc.gpsimd.memset(onesr[:], 1.0).then_inc(consts, 1)
            eye(ident[:], [[-1, P]], 0, 1).then_inc(consts, 1)
            eye(identb[:], [[-1, P]], 0, 2).then_inc(consts, 1)
            eye(selA[:].rearrange("p (j i) -> p j i", i=32), [[-32, 4], [0, 32]], -D0, 3).then_inc(consts, 1)
            for n in range(4):
                eye(eye32[:], [[0, 4], [-1, RANK]], -RANK * n, 11 + n).then_inc(consts, 1)

            def load_ctx(b):
                apart(pool)
                pool.dma_start(C[:], ctxT[bass.ds(b, 1), :, :].rearrange("o (c p) n -> p (o c) n", p=P)
                               ).then_inc(ctx_loaded, 16)

            load_ctx(0)
            with pool.Fori(1, B) as b:
                pool.wait_ge(v_ready, after(b, 4, 0))
                load_ctx(b)

            if "B" in phases:
                pool.wait_ge(v_ready, 4 * B)
                load_ctx(0)
                pool.wait_ge(x_done, XB)
                nc.gpsimd.memset(V1[:, :, :, D1:D1 + 1], 1.0).then_inc(consts_b, 1)
                pool.wait_ge(consts_b, 1)
                nc.gpsimd.memset(K1H[D1:D1 + 2, :, :].bitcast(F32), 1.0).then_inc(consts_b, 1)
                pool.wait_ge(consts_b, 2)
                nc.gpsimd.memset(sel1[0:D1, :], 0.0).then_inc(consts_b, 1)
                pool.wait_ge(consts_b, 3)
                nc.gpsimd.memset(sel1[D1:D1 + 1, :], 1.0).then_inc(consts_b, 1)
                pool.wait_ge(consts_b, 4)
                nc.gpsimd.iota(rank[:], pattern=[[-1, E1]], base=E1, channel_multiplier=0,
                               allow_small_or_imprecise_dtypes=True).then_inc(consts_b, 1)

                def load_wo(g):
                    apart(pool)
                    pool.dma_start(Wo1[:, g % 2, :, :],
                                   wo1[g * J * D1:(g + 1) * J * D1, :].rearrange("(j d) n -> d j n", d=D1)
                                   ).then_inc(wo_loaded[g % 2], 16)

                def load_outputs(b):
                    pool.wait_ge(x_done, after(b, 2, 0, XB))
                    load_wo(0)
                    load_wo(1)
                    for g in range(2, G1):
                        pool.wait_ge(item_ready, after(b, NI, where[("Y", g - 2, QT - 1)] + 1))
                        load_wo(g)

                with pool.Fori(0, B - 1) as b:
                    load_outputs(b)
                    pool.wait_ge(item_ready, after(b, NI, where[("K", G1 - 1, NC0)] + 1))
                    load_ctx(b + 1)
                load_outputs(B - 1)

        @block.tensor
        def _(te):
            def turn_xn(b, L, base, bank):
                te.wait_ge(xn_ready, after(b, 4, 2 * L + 2, base * 4))
                for c in range(KC):
                    for qt in range(QT):
                        at = (c % 2) * Q + qt * P
                        mm = te.transpose(PS[:, bank + c // 2, at:at + P], XN[:, qt, c * P:(c + 1) * P], ident[:])
                mm.then_inc(xnt_ready, 1)
                te.wait_ge(xnt_copied, after(b, 4, 2 * L + 2, base * 4))

            te.wait_ge(consts, 15)
            te.wait_ge(loaded_kv, 32)
            with te.Fori(0, B) as b:
                te.wait_ge(x_done, after(b, 4, 0, 1))
                te.wait_ge(ctx_loaded, after(b, 16, 16))
                for c, (s, w) in enumerate(CH0):
                    for k in range(KC):
                        mm = te.matmul(PS[:, c, 0:w], Wk[:, k, :], C[:, k, s:s + w], start=(k == 0), stop=(k == KC - 1))
                    mm.then_inc(prod_ready, 1)
                for t0 in range(0, len(KT0), 4):
                    for t in range(t0, min(t0 + 4, len(KT0))):
                        s, w = KT0[t]
                        for k in range(KC):
                            mm = te.matmul(PS[0:w, 4 + t0 // 4, (t - t0) * P:(t - t0 + 1) * P], C[:, k, s:s + w],
                                           Wv[:, k, :], start=(k == 0), stop=(k == KC - 1))
                    mm.then_inc(v_ready, 1)
                te.wait_ge(rest_done, after(b, 6, 2))
                turn_xn(b, 0, 0, 0)
                te.wait_ge(loaded_q, 16)
                te.wait_ge(rest_done, after(b, 6, 4))
                for h in range(2):
                    for j in range(2):
                        for k in range(KC):
                            mm = te.matmul(PS[:, 2 + h, j * Q:(j + 1) * Q], Wq[:, k, (2 * h + j) * P:(2 * h + j + 1) * P],
                                           XNT[:, k, :], start=(k == 0), stop=(k == KC - 1))
                    mm.then_inc(prod_ready, 1)

                def score_piece(n):
                    g, i = divmod(n, NS)
                    row, c = divmod(i, NC0)
                    s, w = CH0[c]
                    if n >= 2:
                        te.wait_ge(max_done, after(b, G0 * NS, n - 1))
                    te.matmul(PS[:, n % 2, 0:w], QX[0:R0, g, row * P:(row + 1) * P], KX[0:R0, g, s:s + w],
                              start=True, stop=True).then_inc(s_ready, 1)

                def turn_max(g):
                    te.wait_ge(nm_ready, after(b, G0, g + 1))
                    te.transpose(PS[0:ROWS, 0, 0:P], nm[:], ident[:]).then_inc(nmt_ready, 1)
                    te.wait_ge(nmt_split, after(b, 2 * G0, 2 * g + 2))

                def scores_t(g, t, h):
                    n = g * len(KT0) + t
                    s, w = KT0[t]
                    if n >= 2 and h == 0:
                        te.wait_ge(exp_done, after(b, G0 * len(KT0), n - 1))
                    if t == 0 and h == 0:
                        te.wait_ge(m_rows, after(b, 32 * G0, 32 * (g + 1)))
                    o = PS[0:w, 2 + 2 * (n % 2) + h, :]
                    te.matmul(o, KX[:, g, s:s + w], QX[:, g, h * BANK:(h + 1) * BANK], start=True, stop=False)
                    mm = te.matmul(o, identb[0:w, 0:w],
                                   mT[0:w, t, :].unsqueeze(1).to_broadcast([w, 2, Q]), start=False, stop=True)
                    if h == 1:
                        mm.then_inc(st_ready, 1)

                def values(g, t):
                    n = g * len(KT0) + t
                    s, w = KT0[t]
                    te.wait_ge(exp_done, after(b, G0 * len(KT0), n + 1))
                    if t == 0 and g >= 2:
                        te.wait_ge(rec_done, after(b, G0, g - 1))
                    for j in range(J):
                        mm = te.matmul(PS[32 * j:32 * j + 32, 6 + g % 2, 0:Q], VX[0:w, t, g, :],
                                       PT[0:w, n % 2, j * Q:(j + 1) * Q], start=(t == 0), stop=(t == len(KT0) - 1))
                    mm.then_inc(pv_done, 1)

                def denominators(g):
                    te.wait_ge(o_copied, after(b, G0, g + 1))
                    te.matmul(PS[:, 6 + g % 2, Q:2 * Q], selA[:], OS[:, g % 2, :], start=True, stop=True
                              ).then_inc(den_ready, 1)

                te.wait_ge(k_stacked, after(b, 16 * 6, 16 * 6))
                te.wait_ge(q_stacked, after(b, 16 * 6, 16 * 6))
                te.wait_ge(masks_made, 2)
                te.wait_ge(v_copied, after(b, 4, 4))
                for n in range(NS):
                    score_piece(n)
                turn_max(0)
                for g in range(G0):
                    scores_t(g, 0, 0)
                    scores_t(g, 0, 1)
                    for t in range(len(KT0)):
                        for h in range(3):
                            n = 3 * t + h
                            if g + 1 < G0 and n < NS:
                                score_piece((g + 1) * NS + n)
                            if g + 1 < G0 and n == NS:
                                turn_max(g + 1)
                            if h < 2 and t + 1 < len(KT0):
                                scores_t(g, t + 1, h)
                        values(g, t)
                        if t == 1 and g >= 1:
                            denominators(g - 1)
                denominators(G0 - 1)

                te.wait_ge(loaded_rest, 16 * 11)
                te.wait_ge(on_ready, after(b, G0, G0))
                for qt in range(QT):
                    for g in range(G0):
                        mm = te.matmul(PS[:, qt, :], ON[:, g, qt * P:(qt + 1) * P], WoX[:, g, :],
                                       start=(g == 0), stop=(g == G0 - 1))
                    mm.then_inc(y_ready, 1)
                turn_xn(b, 1, 0, 2)
                for c in range(4):
                    for k in range(KC):
                        mm = te.matmul(PS[:, 4 + c // 2, (c % 2) * Q:(c % 2 + 1) * Q], LA[:, k, c * P:(c + 1) * P],
                                       XNT[:, k, :], start=(k == 0), stop=(k == KC - 1))
                    if c % 2:
                        mm.then_inc(ax_ready, 1)
                for k in range(KC):
                    mm = te.matmul(PS[0:RANK, 6, 0:Q], SA[:, k, :], XNT[:, k, :], start=(k == 0), stop=(k == KC - 1))
                mm.then_inc(ax_ready, 1)
                te.wait_ge(rp_ready, after(b, 1, 1))
                te.wait_ge(ax_copied, after(b, 3, 3))
                for qt in range(QT):
                    for c in range(4):
                        mm = te.matmul(PS[:, 7 if qt else 4, 0:P], RP[:, qt * 4 + c, :], AXA[:, c, qt * P:(qt + 1) * P],
                                       start=(c == 0), stop=(c == 3))
                    mm.then_inc(rep_ready, 1)
                te.wait_ge(x_done, after(b, 4, 2, 1))
                for qt in range(QT):
                    o, rows = PS[:, qt, :], slice(qt * P, (qt + 1) * P)
                    for k in range(KC):
                        te.matmul(o, XNT[:, k, rows], Wd[:, k, :], start=(k == 0), stop=False)
                    te.matmul(o, AXS[:, rows], SB[:], start=False, stop=False)
                    te.matmul(o, onesr[:], biasr[:], start=False, stop=False)
                    te.wait_ge(ga_ready, after(b, 2, qt + 1))
                    for c in range(4):
                        mm = te.matmul(o, GA[:, qt, c, :], LB[:, c, :], start=False, stop=(c == 3))
                    mm.then_inc(y_ready, 1)

            if "B" not in phases:
                return
            te.wait_ge(loaded_b1, 48)
            te.wait_ge(loaded_b2, 48)
            te.wait_ge(consts_b, 5)
            with te.Fori(0, B) as b:
                te.wait_ge(x_done, after(b, 2, 0, XB))
                te.wait_ge(ctx_loaded, after(b, 16, 16, 16 * B))
                T1 = len(KT1)

                def v_tile(n, t):
                    s, w = KT1[t]
                    if n >= 4:
                        te.wait_ge(v1_copied, after(b, T1, n - 3))
                    for k in range(KC):
                        lhs = XNT[:, k, s:s + w] if s < Q else C[:, k, s - Q:s - Q + w]
                        mm = te.matmul(PS[0:w, 2 + n % 4, 0:G1 * D1], lhs, Wv1[:, k, :], start=(k == 0), stop=(k == KC - 1))
                    mm.then_inc(v1_ready, 1)

                for n in range(T1 - QT):
                    v_tile(n, n + QT)
                turn_xn(b, 0, B, 6)
                for n in range(T1 - QT, T1):
                    v_tile(n, n - (T1 - QT))

                def item(n):
                    kind, g, i = items[n]
                    if n >= 2:
                        te.wait_ge(item_done, after(b, NI, n - 1))
                    bank = n % 2
                    if kind == "K":
                        s, w = (0, Q) if i == 0 else (Q + CH0[i - 1][0], CH0[i - 1][1])
                        for k in range(KC):
                            rhs = XNT[:, k, :] if i == 0 else C[:, k, s - Q:s - Q + w]
                            mm = te.matmul(PS[0:D1, bank, 0:w], Wk1[:, k, g * D1:(g + 1) * D1], rhs,
                                           start=(k == 0), stop=(k == KC - 1))
                    elif kind == "Q":
                        for j in range(2):
                            h = g * J + 2 * i + j
                            for k in range(KC):
                                mm = te.matmul(PS[0:D1, bank, j * Q:(j + 1) * Q], Wq1[:, k, h * D1:(h + 1) * D1],
                                               XNT[:, k, :], start=(k == 0), stop=(k == KC - 1))
                    elif kind == "S":
                        row, c = divmod(i, NC0)
                        s, w = CH1[c]
                        if i == 0:
                            te.wait_ge(item_done, after(b, NI, n))
                        mm = te.matmul(PS[:, bank, 0:w], Q1H[0:D1, g % 2, row * P:(row + 1) * P],
                                       K1H[0:D1, g % 2, s:s + w], start=True, stop=True)
                    elif kind == "M":
                        te.wait_ge(nm_ready, after(b, G1, g + 1, G0 * B))
                        mm = te.transpose(PS[0:ROWS, bank, 0:P], nm[:], ident[:])
                    elif kind == "D":
                        te.wait_ge(o1_copied, after(b, G1, g + 1))
                        mm = te.matmul(PS[0:D1, bank, :], sel1[:], OS1[:, i * BANK:(i + 1) * BANK], start=True, stop=True)
                    else:
                        te.wait_ge(item_done, after(b, NI, where[("D", g, 1)] + 1))
                        te.wait_ge(wo_loaded[g % 2], after(b, 16 * G1 // 2, 16 * (g // 2 + 1)))
                        for j in range(J):
                            mm = te.matmul(PS[:, bank, :], ON1[:, j * Q + i * P:j * Q + (i + 1) * P], Wo1[:, g % 2, j, :],
                                           start=(j == 0), stop=(j == J - 1))
                    mm.then_inc(item_ready, 1)

                def scores_t1(g, t, h):
                    n = g * T1 + t
                    s, w = KT1[t]
                    if n >= 2 and h == 0:
                        te.wait_ge(exp1_done, after(b, NP1, n - 1))
                    if t == 0 and h == 0:
                        te.wait_ge(m_rows, after(b, 32 * G1, 32 * (g + 1), 32 * G0 * B))
                    o, cols = PS[0:w, 2 + 2 * (n % 2) + h, :], slice(h * BANK, (h + 1) * BANK)
                    te.matmul(o, K1H[:, g % 2, s:s + w], Q1H[:, g % 2, cols], start=True, stop=False)
                    te.matmul(o, K1H[0:D1, g % 2, s:s + w], Q1L[:, g % 2, cols], start=False, stop=False)
                    mm = te.matmul(o, K1L[:, g % 2, s:s + w], Q1H[0:D1, g % 2, cols], start=False, stop=True)
                    if h == 1:
                        mm.then_inc(st1_ready, 1)

                def values1(g, t, h):
                    n = g * T1 + t
                    s, w = KT1[t]
                    if h == 0:
                        te.wait_ge(exp1_done, after(b, NP1, n + 1))
                        if t == 0 and g >= 1:
                            te.wait_ge(o1_copied, after(b, G1, g))
                    mm = te.matmul(PS[0:D1 + 1, 6 + h, :], V1[0:w, t, g, :], PT[0:w, n % 2, h * BANK:(h + 1) * BANK],
                                   start=(t == 0), stop=(t == T1 - 1))
                    if h == 1:
                        mm.then_inc(pv1_done, 1)

                n_out = where[("M", 0, 0)] + 1
                for n in range(n_out):
                    item(n)
                te.wait_ge(v1_copied, after(b, T1, T1))
                for g in range(G1):
                    scores_t1(g, 0, 0)
                    scores_t1(g, 0, 1)
                    for t in range(T1):
                        due = list(range(*step_items(g, t)))
                        for h in range(4):
                            for n in due[h:h + 1] if h < 3 else due[3:]:
                                item(n)
                            if h < 2 and t + 1 < T1:
                                scores_t1(g, t + 1, h)
                            if h >= 2:
                                values1(g, t, h - 2)
                n_out = window_end[G1 - 1]
                for n in range(n_out, NI):
                    item(n)

                turn_xn(b, 1, B, 2)
                for qt in range(QT):
                    for k in range(KC):
                        mm = te.matmul(PS[:, 4 + qt, 0:P + E1], XNT[:, k, qt * P:(qt + 1) * P], WR[:, k, :],
                                       start=(k == 0), stop=(k == KC - 1))
                    mm.then_inc(h_ready, 1)
                for qt in range(QT):
                    te.wait_ge(wh_ready, after(b, 2, qt + 1))
                    mm = te.transpose(PS[:, 6, qt * P:(qt + 1) * P], WH[:, qt, :], ident[:])
                mm.then_inc(wht_ready, 1)
                te.wait_ge(wht_copied, after(b, 1, 1))
                for qt in range(QT):
                    te.matmul(PS[:, 4 + qt, :], WHT[:, qt * P:(qt + 1) * P], WB[:], start=True, stop=True
                              ).then_inc(y_ready, 1)

        @block.scalar
        def _(ae):
            def root(b, L, base):
                ae.wait_ge(var_ready, after(b, 2, L + 1, base * 2))
                ae.activation(std[:], vpe[:], ACT.Sqrt).then_inc(std_ready, 1)

            def copy_xnt(b, L, base, bank):
                ae.wait_ge(xnt_ready, after(b, 2, L + 1, base * 2))
                for h in range(2):
                    ae.copy(XNT[:, 2 * h:2 * h + 2, :].rearrange("p c q -> p (c q)"), PS[:, bank + h, :]
                            ).then_inc(xnt_copied, 1)

            ae.wait_ge(loaded_gates, 32)
            ae.activation(tg[:], gates[:], ACT.Tanh).then_inc(tanh_done, 1)
            with ae.Fori(0, B) as b:
                ae.wait_ge(x_done, after(b, 4, 0, 1))

                def split_hi(n):
                    ae.wait_ge(prod_ready, after(b, 6, n + 1))
                    w = CH0[n][1] if n < 4 else BANK
                    ae.copy(split_part(n, 0), PS[:, n if n < 4 else n - 2, 0:w]).then_inc(hi_done, 1)

                def split_mid(n):
                    ae.wait_ge(rest_done, after(b, 6, n + 1))
                    w = CH0[n][1] if n < 4 else BANK
                    ae.copy(split_part(n, 1), RS[:, n % 2, 0:w]).then_inc(mid_done, 1)

                root(b, 0, 0)
                for n in range(4):
                    split_hi(n)
                    split_mid(n)
                for q4 in range(4):
                    ae.wait_ge(v_ready, after(b, 4, q4 + 1))
                    nt = min(4, len(KT0) - 4 * q4)
                    w = KT0[4 * q4][1]
                    if q4 == 0:
                        ae.wait_ge(consts, 6)
                    for t in range(nt):
                        cp = ae.copy(VX[0:w, 4 * q4 + t, :, 0:D0],
                                     PS[0:w, 4 + q4, t * P:(t + 1) * P].rearrange("p (g d) -> p g d", d=D0))
                    cp.then_inc(v_copied, 1)
                copy_xnt(b, 0, 0, 0)
                for n in (4, 5):
                    split_hi(n)
                    split_mid(n)
                for g in range(G0):
                    for t, (s, w) in enumerate(KT0):
                        n = g * len(KT0) + t
                        ae.wait_ge(st_ready, after(b, G0 * len(KT0), n + 1))
                        if n >= 2:
                            ae.wait_ge(pv_done, after(b, G0 * len(KT0), n - 1))
                        ae.activation(PT[0:w, n % 2, :], PS[0:w, 2 + 2 * (n % 2):4 + 2 * (n % 2), :].rearrange("p a n -> p (a n)"),
                                      ACT.Exp, scale=D0 ** -0.5).then_inc(exp_done, 1)
                        if t == 0 and g >= 1:
                            copy_out(b, g - 1)
                copy_out(b, G0 - 1)
                root(b, 1, 0)
                copy_xnt(b, 1, 0, 2)
                for h in range(2):
                    ae.wait_ge(ax_ready, after(b, 3, h + 1))
                    ae.copy(AXA[:, 2 * h:2 * h + 2, :].rearrange("p c q -> p (c q)"), PS[:, 4 + h, :]).then_inc(ax_copied, 1)
                ae.wait_ge(ax_ready, after(b, 3, 3))
                ae.copy(AXS[:], PS[0:RANK, 6, 0:Q]).then_inc(ax_copied, 1)

            if "B" not in phases:
                return
            with ae.Fori(0, B) as b:
                T1 = len(KT1)
                ae.wait_ge(x_done, after(b, 2, 0, XB))

                def copy_v(n, t):
                    w = KT1[t][1]
                    ae.wait_ge(v1_ready, after(b, T1, n + 1))
                    ae.copy(V1[0:w, t, :, 0:D1], PS[0:w, 2 + n % 4, 0:G1 * D1].rearrange("p (g d) -> p g d", d=D1)
                            ).then_inc(v1_copied, 1)

                def item_half(n):
                    kind, g, i = items[n]
                    ae.wait_ge(item_ready, after(b, NI, n + 1))
                    dst, w = half_of(n, K1H, Q1H)
                    ae.copy(dst, PS[0:D1, n % 2, 0:w]).then_inc(item_hi, 1)

                root(b, 0, B)
                ae.wait_ge(consts_b, 1)
                for n in range(T1 - QT):
                    copy_v(n, n + QT)
                copy_xnt(b, 0, B, 6)
                for n in range(T1 - QT, T1):
                    copy_v(n, n - (T1 - QT))
                def halves(start, end):
                    for n in range(start, end):
                        if items[n][0] in "KQ":
                            item_half(n)

                halves(0, where[("M", 0, 0)])
                for g in range(G1):
                    for t, (s, w) in enumerate(KT1):
                        n = g * T1 + t
                        ae.wait_ge(st1_ready, after(b, NP1, n + 1))
                        if n >= 2:
                            ae.wait_ge(pv1_done, after(b, NP1, n - 1))
                        ae.activation(PT[0:w, n % 2, :], PS[0:w, 2 + 2 * (n % 2):4 + 2 * (n % 2), :].rearrange("p a n -> p (a n)"),
                                      ACT.Exp, scale=D1 ** -0.5).then_inc(exp1_done, 1)
                        if t == 0 and g >= 1:
                            copy_out1(b, g - 1)
                        if t >= 1:
                            halves(*step_items(g, t - 1))
                    halves(*step_items(g, T1 - 1))
                copy_out1(b, G1 - 1)
                root(b, 1, B)
                copy_xnt(b, 1, B, 2)
                ae.wait_ge(wht_ready, after(b, 1, 1))
                ae.copy(WHT[:], PS[:, 6, 0:Q]).then_inc(wht_copied, 1)

        @block.vector
        def _(ve):
            def layer_norm(b, L, base):
                s0 = 5 * L
                for qt in range(QT):
                    apart(ve)
                    ve.bn_stats(stats[:, qt, :], xt(b, qt)).then_inc(ln_step, 1)
                ve.wait_ge(ln_step, after(b, 10, s0 + 2, base * 10))
                for qt in range(QT):
                    apart(ve)
                    ve.bn_aggr(mv[:, qt, :], stats[:, qt, :]).then_inc(ln_step, 1)
                ve.wait_ge(ln_step, after(b, 10, s0 + 4, base * 10))
                ve.tensor_scalar(vpe[:], mv[:, :, 1], EPS, None, ALU.add).then_inc(var_ready, 1)
                ve.wait_ge(std_ready, after(b, 2, L + 1, base * 2))
                ve.reciprocal(rstd[:], std[:]).then_inc(ln_step, 1)
                ve.wait_ge(ln_step, after(b, 10, s0 + 5, base * 10))
                for qt in range(QT):
                    ve.tensor_scalar(XN[:, qt, :], xt(b, qt), mv[:, qt, 0:1], rstd[:, qt:qt + 1],
                                     ALU.subtract, ALU.mult).then_inc(xn_ready, 1)

            ve.sem_inc(x_done, 1)
            ve.wait_ge(loaded_mask, 48)
            ve.tensor_scalar(mq[:], m8, -MASKED, MASKED, ALU.mult, ALU.add).then_inc(masks_made, 1)
            full = N0 // P
            ve.tensor_scalar(mT[:, 0:full, :], mT8[:, 0:full, :], -MASKED, MASKED, ALU.mult, ALU.add)
            ve.tensor_scalar(mT[0:N0 - full * P, full, :], mT8[0:N0 - full * P, full, :], -MASKED, MASKED,
                             ALU.mult, ALU.add).then_inc(masks_made, 1)
            ve.wait_ge(masks_made, 2)
            ve.wait_ge(loaded_x, 16)
            ve.wait_ge(loaded_rest, 16 * 11)
            ve.wait_ge(tanh_done, 1)
            ve.wait_ge(consts, 15)
            with ve.Fori(0, B) as b:
                ve.wait_ge(x_done, after(b, 4, 0, 1))

                def split_rest(n):
                    ve.wait_ge(hi_done, after(b, 6, n + 1))
                    if n >= 2:
                        ve.wait_ge(lo_done, after(b, 6, n - 1))
                    w = CH0[n][1] if n < 4 else BANK
                    ve.tensor_tensor(RS[:, n % 2, 0:w], PS[:, n if n < 4 else n - 2, 0:w], split_part(n, 0),
                                     ALU.subtract).then_inc(rest_done, 1)

                def split_lo(n):
                    ve.wait_ge(mid_done, after(b, 6, n + 1))
                    w = CH0[n][1] if n < 4 else BANK
                    ve.tensor_tensor(split_part(n, 2), RS[:, n % 2, 0:w], split_part(n, 1),
                                     ALU.subtract).then_inc(lo_done, 1)

                def max_piece(n):
                    g, i = divmod(n, NS)
                    row, c = divmod(i, NC0)
                    s, w = CH0[c]
                    ve.wait_ge(s_ready, after(b, G0 * NS, n + 1))
                    if n >= 2:
                        ve.wait_ge(max_done, after(b, G0 * NS, n - 1))
                    apart(ve)
                    ve.tensor_tensor_reduce(junk[:, n % 2, 0:w], PS[:, n % 2, 0:w], mq[:, row % QT, s:s + w], 1.0,
                                            MASKED, ALU.add, ALU.max, pm[:, row, c:c + 1]).then_inc(max_done, 1)

                def row_max(g):
                    ve.wait_ge(max_done, after(b, G0 * NS, (g + 1) * NS))
                    if g >= 1:
                        ve.wait_ge(nmt_ready, after(b, G0, g))
                    ve.tensor_reduce(nm[:], pm[:], AX.X, ALU.max, negate=True).then_inc(nm_ready, 1)
                    ve.wait_ge(nmt_ready, after(b, G0, g + 1))
                    if g >= 1:
                        ve.wait_ge(m_rows, after(b, 32 * G0, 32 * g))
                    ve.tensor_copy(NMT[:, 0, :], PS[0:ROWS, 0, 0:P]).then_inc(nmt_split, 1)
                    ve.wait_ge(nmt_split, after(b, 2 * G0, 2 * g + 1))
                    ve.tensor_tensor(NMT[:, 1, :], PS[0:ROWS, 0, 0:P], NMT[:, 0, :], ALU.subtract).then_inc(nmt_split, 1)

                def normalise(g):
                    ve.wait_ge(den_ready, after(b, G0, g + 1))
                    if g >= 1:
                        ve.wait_ge(on_ready, after(b, G0, g))
                    ve.reciprocal(RC[:], PS[:, 6 + g % 2, Q:2 * Q]).then_inc(rec_done, 1)
                    ve.wait_ge(rec_done, after(b, G0, g + 1))
                    ve.tensor_tensor(ON[:, g, :], OS[:, g % 2, :], RC[:], ALU.mult).then_inc(on_ready, 1)

                layer_norm(b, 0, 0)
                for n in range(5):
                    if n < 4:
                        split_rest(n)
                    if n >= 1:
                        split_lo(n - 1)
                for n in (4, 5):
                    split_rest(n)
                    split_lo(n)
                for n in range(NS):
                    max_piece(n)
                row_max(0)
                for g in range(G0):
                    n_out = (g + 1) * NS
                    for t in range(len(KT0)):
                        if g + 1 < G0:
                            upto = min((g + 1) * NS + 3 * (t + 1), (g + 2) * NS)
                            for n in range(n_out, upto):
                                max_piece(n)
                            if upto == (g + 2) * NS and n_out < upto:
                                row_max(g + 1)
                            n_out = max(n_out, upto)
                        if t == 1 and g >= 1:
                            normalise(g - 1)
                normalise(G0 - 1)
                ve.tensor_tensor(RP, eye32[:].rearrange("p r k -> p (r k)").unsqueeze(1).to_broadcast([P, QT * 4, P]),
                                 gcol[:, bass.ds(b * (QT * 4), QT * 4)].unsqueeze(2).to_broadcast([P, QT * 4, P]),
                                 ALU.mult).then_inc(rp_ready, 1)
                for qt in range(QT):
                    ve.wait_ge(y_ready, after(b, 4, qt + 1))
                    ve.scalar_tensor_tensor(xt(b, qt), PS[:, qt, :], tg[:, 0:1], xt(b, qt), ALU.mult, ALU.add
                                            ).then_inc(x_done, 1)
                ve.wait_ge(x_done, after(b, 4, 2, 1))
                layer_norm(b, 1, 0)
                for qt in range(QT):
                    ve.wait_ge(rep_ready, after(b, 2, qt + 1))
                    ve.tensor_tensor(GA[:, qt, :, :], PS[:, 7 if qt else 4, 0:P].unsqueeze(1).to_broadcast([P, 4, P]),
                                     gcol[:, bass.ds(b * (QT * 4) + qt * 4, 4)].unsqueeze(2).to_broadcast([P, 4, P]),
                                     ALU.mult).then_inc(ga_ready, 1)
                for qt in range(QT):
                    ve.wait_ge(y_ready, after(b, 4, 2 + qt + 1))
                    ve.scalar_tensor_tensor(xt(b, qt), PS[:, qt, :], tg[:, 2:3], xt(b, qt), ALU.mult, ALU.add
                                            ).then_inc(x_done, 1)
                
            if "B" not in phases:
                return
            ve.wait_ge(consts_b, 5)
            with ve.Fori(0, B) as b:
                ve.wait_ge(x_done, after(b, 2, 0, XB))

                def item(n):
                    kind, g, i = items[n]
                    bank = n % 2
                    ve.wait_ge(item_ready, after(b, NI, n + 1))
                    if kind in "KQ":
                        ve.wait_ge(item_hi, after(b, NHI, hi_order[items[n]] + 1))
                        hi, w = half_of(n, K1H, Q1H)
                        ve.tensor_tensor(half_of(n, K1L, Q1L)[0], PS[0:D1, bank, 0:w], hi.bitcast(F32),
                                         ALU.subtract).then_inc(item_done, 1)
                    elif kind == "S":
                        row, c = divmod(i, NC0)
                        ve.tensor_reduce(pm[:, row, c:c + 1], PS[:, bank, 0:CH1[c][1]], AX.X, ALU.max).then_inc(item_done, 1)
                        if i == NS - 1:
                            ve.wait_ge(item_done, after(b, NI, n + 1))
                            if g >= 1:
                                ve.wait_ge(item_ready, after(b, NI, where[("M", g - 1, 0)] + 1))
                            ve.tensor_reduce(nm[:], pm[:], AX.X, ALU.max, negate=True).then_inc(nm_ready, 1)
                    elif kind == "M":
                        if g >= 1:
                            ve.wait_ge(m_rows, after(b, 32 * G1, 32 * g, 32 * G0 * B))
                        ve.tensor_copy(NMT1[:, 0, :], PS[0:ROWS, bank, 0:P]).then_inc(nmt_split, 1)
                        ve.wait_ge(nmt_split, after(b, 2 * G1, 2 * g + 1, 2 * G0 * B))
                        ve.tensor_tensor(NMT1[:, 1, :], PS[0:ROWS, bank, 0:P], NMT1[:, 0, :].bitcast(F32),
                                         ALU.subtract).then_inc(nmt_split, 1)
                        ve.wait_ge(nmt_split, after(b, 2 * G1, 2 * g + 2, 2 * G0 * B))
                        ve.sem_inc(item_done, 1)
                    elif kind == "D":
                        cols = slice(i * BANK, (i + 1) * BANK)
                        ve.reciprocal(RC1[:, cols], PS[0:D1, bank, :]).then_inc(rec1_done, 1)
                        ve.wait_ge(rec1_done, after(b, 2 * G1, 2 * g + i + 1))
                        ve.tensor_tensor(ON1[:, cols], OS1[0:D1, cols], RC1[:, cols], ALU.mult).then_inc(item_done, 1)
                    else:
                        if g >= 1:
                            ve.wait_ge(item_done, after(b, NI, where[("Y", g - 1, i)] + 1))
                        ve.scalar_tensor_tensor(xt(b, i), PS[:, bank, :], tg[:, 1:2], xt(b, i), ALU.mult, ALU.add
                                                ).then_inc(item_done, 1)

                layer_norm(b, 0, B)
                for n in range(NI):
                    item(n)
                ve.wait_ge(item_done, after(b, NI, NI))
                layer_norm(b, 1, B)
                R = lambda qt, k: ve.wait_ge(rt_step, after(b, 10, 5 * qt + k))
                for qt in range(QT):
                    h, lg = PS[:, 4 + qt, 0:P], PS[:, 4 + qt, P:P + E1]
                    ve.wait_ge(h_ready, after(b, 2, qt + 1))
                    ve.tensor_reduce(top[:, qt, 0:1], lg, AX.X, ALU.max).then_inc(rt_step, 1)
                    R(qt, 1)
                    ve.tensor_scalar(lgt[:, qt, 0, :], lg, top[:, qt, 0:1], None, ALU.is_equal).then_inc(rt_step, 1)
                    R(qt, 2)
                    ve.tensor_tensor(lgt[:, qt, 1, :], lgt[:, qt, 0, :], rank[:], ALU.mult).then_inc(rt_step, 1)
                    R(qt, 3)
                    ve.tensor_reduce(top[:, qt, 1:2], lgt[:, qt, 1, :], AX.X, ALU.max).then_inc(rt_step, 1)
                    R(qt, 4)
                    ve.tensor_scalar(lgt[:, qt, 2, :], rank[:], top[:, qt, 1:2], top[:, qt, 0:1], ALU.is_equal, ALU.mult
                                     ).then_inc(rt_step, 1)
                    R(qt, 5)
                    ve.tensor_tensor(WH[:, qt, :].rearrange("p (e r) -> p e r", e=E1), h.rearrange("p (e r) -> p e r", e=E1),
                                     lgt[:, qt, 2, :].unsqueeze(2).to_broadcast([P, E1, RK1]), ALU.mult).then_inc(wh_ready, 1)
                for qt in range(QT):
                    ve.wait_ge(y_ready, after(b, 2, qt + 1, 4 * B))
                    ve.scalar_tensor_tensor(xt(b, qt), PS[:, 4 + qt, :], tg[:, 3:4], xt(b, qt), ALU.mult, ALU.add
                                            ).then_inc(x_done, 1)
                

def lay_out(i):
    import numpy as np

    a = {k: np.asarray(v) for k, v in i.items()}
    c = np.ascontiguousarray
    D = a["x"].shape[-1]
    mask = a["mask_SxS2_bk0"]
    wq = a["L0_xattn_w_q"].reshape(8, 4, 16, D)
    r = a["L0_ffn_lora_A"].shape[1]
    return {
        "x": c(a["x"].reshape(-1, D)),
        "ctxT": c(a["ctx_4096"].transpose(0, 2, 1)),
        "mask": c(mask),
        "maskT": c(mask.T),
        "g_xattn": c(a["g_xattn"]),
        "g_ffn": c(a["g_ffn"]),
        "wq0": c(wq.transpose(3, 1, 0, 2).reshape(D, -1)),
        "wk0": c(a["L0_xattn_w_k"].T),
        "wv0": c(a["L0_xattn_w_v"].T),
        "wo0": c(a["L0_xattn_w_out"].T),
        "gate_rep": c(np.repeat(a["L0_ffn_gate"].T, r, axis=0).reshape(4, 128, -1).transpose(1, 2, 0).reshape(128, -1)),
        "dense": c(a["L0_ffn_kernel"]),
        "bias": c(a["L0_ffn_bias"].reshape(1, -1)),
        "loraA": c(a["L0_ffn_lora_A"].reshape(-1, D).T),
        "loraB": c(a["L0_ffn_lora_B"].transpose(0, 2, 1).reshape(-1, D)),
        "sharedA": c(a["L0_ffn_lora_A_shared"].T),
        "sharedB": c(a["L0_ffn_lora_B_shared"].T),
        "wq1": c(a["L1_xattn_Wq"].T),
        "wk1": c(a["L1_xattn_Wk"].T),
        "wv1": c(a["L1_xattn_Wv"].T),
        "wo1": c(a["L1_xattn_Wo"].T),
        "routeT": c(a["L1_ffn_route_w"].T),
        "expertA": c(a["L1_ffn_A"].reshape(-1, D).T),
        "expertB": c(a["L1_ffn_Bw"].transpose(0, 2, 1).reshape(-1, D)),
    }


def kernel(**inputs):
    import numpy as np
    import concourse.bacc as bacc
    from concourse.bass_utils import run_bass_kernel_spmd

    nc = bacc.Bacc("TRN2", target_bir_lowering=False, num_devices=1)
    arrays = {f"in_{k}": v for k, v in lay_out(inputs).items()}
    args = [nc.dram_tensor(k, v.shape, mybir.dt.from_np(v.dtype), kind="ExternalInput").ap()
            for k, v in arrays.items()]
    shape = np.asarray(inputs["x"]).shape
    out = nc.dram_tensor("out_x", (shape[0] * shape[1], shape[2]), F32, kind="ExternalOutput").ap()
    flamingo_kernel(nc, *args, out)
    r = run_bass_kernel_spmd(nc, [arrays], core_ids=[0])
    return r.results[0]["out_x"].reshape(shape)
```

```python
from contextlib import ExitStack

import concourse.bass as bass
from concourse import mybir

ALU = mybir.AluOpType
ACT = mybir.ActivationFunctionType
AX = mybir.AxisListType
F32 = mybir.dt.float32
F32R = mybir.dt.float32r
BF16 = mybir.dt.bfloat16
U8 = mybir.dt.uint8

P = 128
BANK = 512
MASKED = -3.3895313892515355e38
EPS = 1e-5


def pieces(total, n):
    base, extra = divmod(total, n)
    out, at = [], 0
    for i in range(n):
        w = base + (i < extra)
        out.append((at, w))
        at += w
    return out


def flamingo_kernel(nc, x, ctxT, mask, maskT, g_xattn, g_ffn, wq0, wk0, wv0, wo0, gate_rep, dense,
                    bias, loraA, loraB, sharedA, sharedB, wq1, wk1, wv1, wo1, routeT, expertA,
                    expertB, out, phases="AB"):
    B, D, N0 = ctxT.shape
    Q = x.shape[0] // B
    QT = Q // P
    KC = D // P
    TILES = B * QT
    G0, J, D0 = 8, 4, 16
    HQ = J * Q
    PART_Q, PART_K = (0, 1, 2, 0, 1, 0), (0, 0, 0, 1, 1, 2)
    R0 = len(PART_Q) * D0
    KT0 = [(s, min(P, N0 - s)) for s in range(0, N0, P)]
    CH0 = pieces(N0, 4)
    NC0 = len(CH0)
    RANK, NL = 32, 16
    G1, D1 = 4, 96
    N1 = Q + N0
    KT1 = [(s, P) for s in range(0, Q, P)] + [(Q + s, w) for s, w in KT0]
    CW1 = -(-N1 // 4) + (-(-N1 // 4)) % 2
    CH1 = [(min(i * CW1, N1 - CW1), CW1) for i in range(4)]
    E1, RK1 = 8, 16
    ROWS = J * QT
    NS = ROWS * NC0

    with ExitStack() as ctx:
        def sb(name, shape, dt, to=ctx):
            return to.enter_context(nc.sbuf_tensor(name, shape, dt))

        def sem(name):
            return ctx.enter_context(nc.semaphore(name))

        PS = ctx.enter_context(nc.psum_tensor("PS", [P, 8, BANK], F32))

        X = sb("X", [P, TILES * D], F32)
        C = sb("C", [P, KC, N0], F32)
        ident = sb("ident", [P, P], F32)
        gates = sb("gates", [P, 4], F32)
        tg = sb("tg", [P, 4], F32)
        stats = sb("stats", [P, QT, 6], F32)
        mv = sb("mv", [P, QT, 2], F32)
        vpe = sb("vpe", [P, QT], F32)
        std = sb("std", [P, QT], F32)
        rstd = sb("rstd", [P, QT], F32)
        XN = sb("XN", [P, QT, D], F32)
        XNT = sb("XNT", [P, KC, Q], F32)
        PT = sb("PT", [P, 2, HQ], F32)
        pm = sb("pm", [P, ROWS, NC0], F32)
        nm = sb("nm", [P, ROWS], F32)

        KD = nc.dram_tensor("KD", (3, P, N0), BF16).ap()
        QD = nc.dram_tensor("QD", (3, P, HQ), BF16).ap()

        mA = ExitStack()
        identb = sb("identb", [P, P], BF16, mA)
        selA = sb("selA", [P, 2, P], F32, mA)
        halves = sb("halves", [P, 2], F32, mA)
        eye32 = sb("eye32", [P, 4, RANK], F32, mA)
        onesr = sb("onesr", [1, P], F32, mA)
        Wq = sb("Wq", [P, KC, D], F32, mA)
        Wk = sb("Wk", [P, KC, P], F32, mA)
        Wv = sb("Wv", [P, KC, P], F32, mA)
        WoX = sb("WoX", [P, G0 // 2, D], F32, mA)
        Wd = sb("Wd", [P, KC, D], F32, mA)
        LA = sb("LA", [P, KC, NL * RANK], F32, mA)
        LB = sb("LB", [P, 4, D], F32, mA)
        SA = sb("SA", [P, KC, RANK], F32, mA)
        SB = sb("SB", [RANK, D], F32, mA)
        biasr = sb("biasr", [1, D], F32, mA)
        gcol = sb("gcol", [P, TILES * 4], F32, mA)
        bytes8 = PT[:].rearrange("p a n -> p (a n)").bitcast(U8)
        m8 = bytes8[:, 0:QT * N0].rearrange("p (t n) -> p t n", n=N0)
        mT8 = bytes8[:, QT * N0:QT * N0 + len(KT0) * Q].rearrange("p (t q) -> p t q", q=Q)
        mq = sb("mq", [P, QT, N0], BF16, mA)
        mT = sb("mT", [P, len(KT0), Q], BF16, mA)
        KS = sb("KS", [P, 3, N0 + N0 % 2], BF16, mA)
        QS = sb("QS", [P, 3, HQ], BF16, mA)
        RS = sb("RS", [P, 2, BANK], F32, mA)
        KX = sb("KX", [R0 + 2, G0, N0], BF16, mA)
        QX = sb("QX", [R0 + 2, G0, HQ], BF16, mA)
        VX = sb("VX", [P, len(KT0), G0, 2 * D0], F32, mA)
        NMT = sb("NMT", [ROWS, 2, P], BF16, mA)
        OS = sb("OS", [P, 2, Q], F32, mA)
        RC = sb("RC", [P, Q], F32, mA)
        odd = sb("odd", [P, Q], F32, mA)
        AXS = sb("AXS", [RANK, Q], F32, mA)
        junk = RS[:].bitcast(BF16)
        ON = KS[:].rearrange("p a n -> p (a n)")[:, 0:G0 * Q].bitcast(F32).rearrange("p (g q) -> p g q", q=Q)
        RP = RS[:].rearrange("p a n -> p (a n)").rearrange("p (i k) -> p i k", k=P)
        AXA = PT[:, 0, :].rearrange("p (c q) -> p c q", q=Q)
        GA = PT[:, 1, :].rearrange("p (t c q) -> p t c q", t=QT, c=4)
        mA.close()

        mB = ExitStack()
        one1 = sb("one1", [P, 1], F32, mB)
        Wk1 = sb("Wk1", [P, KC, G1 * D1], F32, mB)
        Wv1 = sb("Wv1", [P, KC, G1 * D1], F32, mB)
        Wq1 = sb("Wq1", [P, KC, G1 * J * D1], F32, mB)
        Wo1 = sb("Wo1", [D1, 2, J, D], F32, mB)
        WR = sb("WR", [P, KC, P + E1], F32, mB)
        WB = sb("WB", [P, D], F32, mB)
        K1H = sb("K1H", [D1 + 2, 2, N1], F32R, mB)
        K1L = sb("K1L", [D1, 2, N1], F32R, mB)
        Q1H = sb("Q1H", [D1 + 2, 2, HQ], F32R, mB)
        Q1L = sb("Q1L", [D1, 2, HQ], F32R, mB)
        V1 = sb("V1", [P, len(KT1), G1, D1 + 1], F32, mB)
        NMT1 = sb("NMT1", [ROWS, 2, P], F32R, mB)
        OS1 = sb("OS1", [D1 + 1, HQ], F32, mB)
        RC1 = sb("RC1", [P, ROWS], F32, mB)
        RG1 = sb("RG1", [P, ROWS], F32, mB)
        top = sb("top", [P, QT, 4], F32, mB)
        lgt = sb("lgt", [P, QT, 4, E1], F32, mB)
        rank = sb("rank", [P, E1], F32, mB)
        WH = sb("WH", [P, QT, P], F32, mB)
        WHT = sb("WHT", [P, Q], F32, mB)
        mB.close()

        spent = sem("spent")
        consts = sem("consts")
        loaded_x = sem("loaded_x")
        loaded_k = sem("loaded_k")
        loaded_v = sem("loaded_v")
        loaded_q = sem("loaded_q")
        loaded_mask = sem("loaded_mask")
        loaded_gates = sem("loaded_gates")
        loaded_rest = sem("loaded_rest")
        masks_made = sem("masks_made")
        tanh_done = sem("tanh_done")
        loaded_ctx = [sem(f"loaded_ctx_{c}") for c in range(NC0)]
        ctx_loaded = sem("ctx_loaded")
        ln_step = [sem("ln1_step"), sem("ln2_step")]
        var_ready = [sem("var1_ready"), sem("var2_ready")]
        std_ready = [sem("std1_ready"), sem("std2_ready")]
        xn_ready = [sem("xn1_ready"), sem("xn2_ready")]
        xnt_ready = [sem("xnt1_ready"), sem("xnt2_ready")]
        xnt_copied = [sem("xnt1_copied"), sem("xnt2_copied")]
        prod_ready = sem("prod_ready")
        hi_done = sem("hi_done")
        rest_done = sem("rest_done")
        mid_done = sem("mid_done")
        lo_done = sem("lo_done")
        v_ready = sem("v_ready")
        v_copied = sem("v_copied")
        k_parked = sem("k_parked")
        k_stacked = sem("k_stacked")
        q_parked = sem("q_parked")
        q_stacked = sem("q_stacked")
        s_ready = sem("s_ready")
        max_done = sem("max_done")
        nm_ready = sem("nm_ready")
        nmt_ready = sem("nmt_ready")
        nmt_split = sem("nmt_split")
        m_rows = sem("m_rows")
        st_ready = sem("st_ready")
        exp_done = sem("exp_done")
        pv_done = sem("pv_done")
        o_copied = sem("o_copied")
        den_ready = sem("den_ready")
        rec_done = sem("rec_done")
        odd_ready = sem("odd_ready")
        on_ready = sem("on_ready")
        y_ready = sem("y_ready")
        x_done = sem("x_done")
        rp_ready = sem("rp_ready")
        ax_ready = sem("ax_ready")
        ax_copied = sem("ax_copied")
        rep_ready = sem("rep_ready")
        ga_ready = sem("ga_ready")
        loaded_v1 = sem("loaded_v1")
        loaded_k1 = sem("loaded_k1")
        loaded_q1 = sem("loaded_q1")
        loaded_b2 = sem("loaded_b2")
        consts_b = sem("consts_b")
        wo_loaded = [sem("wo_loaded_0"), sem("wo_loaded_1")]
        v1_ready = sem("v1_ready")
        v1_copied = sem("v1_copied")
        item_ready = sem("item_ready")
        item_hi = sem("item_hi")
        item_done = sem("item_done")
        st1_ready = sem("st1_ready")
        exp1_done = sem("exp1_done")
        pv1_done = sem("pv1_done")
        o1_copied = sem("o1_copied")
        rec1_done = sem("rec1_done")
        h_ready = sem("h_ready")
        rt_step = sem("rt_step")
        wh_ready = sem("wh_ready")
        wht_ready = sem("wht_ready")
        wht_copied = sem("wht_copied")
        stored = sem("stored")

        def xt(b, qt):
            return X[:, bass.ds(b * (QT * D) + qt * D, D)]

        def after(b, per, k, base=0):
            return b * per + (base + k)

        XB = 4 * B + 1

        def apart(eng):
            eng.sem_inc(spent, 1)

        block = ctx.enter_context(nc.Block())

        def group_items(g):
            return ([("K", g, c) for c in range(1 + NC0)] + [("Q", g, c) for c in range(2)]
                    + [("S", g, i) for i in range(NS)] + [("M", g, 0)])

        def finish_items(g):
            return [("R", g, 0)] + [("Y", g, i) for i in range(ROWS)]

        items = group_items(0)
        window_end = []
        for g in range(G1):
            ahead = group_items(g + 1) if g + 1 < G1 else []
            items += ahead[:2] + (finish_items(g - 1) if g >= 1 else []) + ahead[2:]
            window_end.append(len(items))
        items += finish_items(G1 - 1)
        NI = len(items)
        assert NI % 2 == 0
        where = {it: n for n, it in enumerate(items)}
        NHI = sum(it[0] in "KQ" for it in items)
        hi_order = {it: n for n, it in enumerate([it for it in items if it[0] in "KQ"])}
        NP1 = len(KT1) * G1
        NP0 = len(KT0) * G0
        MAX_STEP = 9
        V_BANK = (0, 1, 4, 5)
        FFN_STEPS = KC + 2 + 4
        assert NP1 % 2 == 0 and (len(KT0) * G0) % 2 == 0

        def step_items(g, t):
            start = where[("M", 0, 0)] + 1 if g == 0 else window_end[g - 1]
            end = window_end[g]

            def upto(t):
                if t < 0:
                    return start + (2 if g == 0 and t == -1 else 0)
                if t == 0 and g >= 1:
                    return start + 2 * (g + 1 < G1)
                return min(start + -(-(end - start) * (t + 1) // (len(KT1) - 3)), end)
            return upto(t - 1), upto(t)

        T1 = len(KT1)
        V_ORDER = list(range(QT, T1 - 3)) + list(range(QT)) + list(range(T1 - 3, T1))
        V_FINISH, V_START = 7, 3
        V_BESIDE = [i for i in range(1, NS) if i % 3][:KC * (T1 - V_FINISH - V_START)]
        V_BESIDE = {i: (V_FINISH + V_START + n // KC, n % KC) for n, i in enumerate(V_BESIDE)}
        assert V_FINISH + V_START <= T1 - 3 - QT and len(V_BESIDE) == KC * (T1 - V_FINISH - V_START)

        def v_bank(n):
            return 2 + (n + 1) % 4

        def a_pieces(g, t):
            after_max = len(KT0) - (MAX_STEP + 2)
            if t < MAX_STEP:
                group, step, steps = g + 1, t + (after_max if g else 0), MAX_STEP + (after_max if g else 0)
            else:
                group, step, steps = g + 2, t - (MAX_STEP + 2), MAX_STEP + after_max
            if group >= G0 or step < 0:
                return []
            return [group * NS + n for n in range(-(-NS * step // steps), -(-NS * (step + 1) // steps))]

        def tail_plan(ffn, nxt):
            work = []
            if ffn:
                work += [("ffn", qt, m) for qt in range(QT) for m in range(FFN_STEPS)]
            if nxt:
                work += [("values", q4, i) for q4 in (2, 3) for i in range(2 * min(4, len(KT0) - 4 * q4))]
            if not nxt:
                return work
            if not ffn:
                return work[:8] + [("piece", 0, n) for n in range(NS)] + [("max", 0, 0)] + work[8:]
            plan, n = [], 0
            for i, step in enumerate(work):
                plan.append(step)
                for _ in range((i >= 3) + (FFN_STEPS <= i < 2 * FFN_STEPS)):
                    if n < NS:
                        plan.append(("piece", 0, n))
                        n += 1
                if i == QT * FFN_STEPS + 5:
                    assert n == NS
                    plan.append(("max", 0, 0))
            return plan

        def split_part(n, part):
            if n < 4:
                s, w = CH0[n]
                return KS[:, part, s:s + w]
            return QS[:, part, (n - 4) * BANK:(n - 3) * BANK]

        def half_of(n, k_tile, q_tile):
            kind, g, i = items[n]
            if kind == "K":
                s, w = (0, Q) if i == 0 else (Q + CH0[i - 1][0], CH0[i - 1][1])
                return k_tile[0:D1, g % 2, s:s + w], w
            return q_tile[0:D1, g % 2, i * BANK:(i + 1) * BANK], BANK

        def copy_out(b, g):
            ae = nc.scalar
            ae.wait_ge(pv_done, after(b, G0 * len(KT0), (g + 1) * len(KT0)))
            if g >= 2:
                ae.wait_ge(on_ready, after(b, G0, g - 1))
            ae.copy(OS[:, g % 2, :], PS[:, 6 + g % 2, 0:Q]).then_inc(o_copied, 1)

        def copy_out1(b, g):
            ae = nc.scalar
            ae.wait_ge(pv1_done, after(b, NP1, (g + 1) * len(KT1)))
            if g >= 1:
                ae.wait_ge(item_ready, after(b, NI, where[("Y", g - 1, ROWS - 1)] + 1))
            ae.copy(OS1[:], PS[0:D1 + 1, 6:8, :].rearrange("p a n -> p (a n)")).then_inc(o1_copied, 1)

        @block.sync
        def _(sp):
            sp.dma_start(Wk[:], wk0.rearrange("(c p) n -> p c n", p=P)).then_inc(loaded_k, 16)
            for c, (s, w) in enumerate(CH0):
                sp.dma_start(C[:, :, s:s + w], ctxT[0, :, s:s + w].rearrange("(c p) n -> p c n", p=P)
                             ).then_inc(loaded_ctx[c], 16)
            sp.dma_start(Wv[:], wv0.rearrange("(c p) n -> p c n", p=P)).then_inc(loaded_v, 16)
            Xb, xb = X[:].rearrange("p (t d) -> p t d", d=D), x.rearrange("(t p) d -> p t d", p=P)
            sp.dma_start(Xb[:, 0:QT, :], xb[:, 0:QT, :]).then_inc(loaded_x, 16)
            sp.dma_start(Wq[:], wq0.rearrange("(c p) n -> p c n", p=P)).then_inc(loaded_q, 16)
            sp.dma_start(gates[:, 0:2], g_xattn.partition_broadcast(P)).then_inc(loaded_gates, 16)
            sp.dma_start(gates[:, 2:4], g_ffn.partition_broadcast(P)).then_inc(loaded_gates, 16)
            sp.dma_start(m8, mask.rearrange("(t p) n -> p t n", p=P)).then_inc(loaded_mask, 16)
            full = N0 // P
            sp.dma_start(mT8[:, 0:full, :], maskT[0:full * P, :].rearrange("(t p) q -> p t q", p=P)
                         ).then_inc(loaded_mask, 16)
            sp.dma_start(mT8[0:N0 - full * P, full, :], maskT[full * P:N0, :]).then_inc(loaded_mask, 16)
            def park_q(b, first):
                if not first:
                    sp.wait_ge(q_stacked, after(b, 16 * 6, 0))
                    apart(sp)
                sp.wait_ge(lo_done, after(b, 6, 6))
                sp.dma_start(QD.rearrange("a p n -> p a n"), QS[:]).then_inc(q_parked, 16)

            def stack(b, first):
                if not first:
                    sp.wait_ge(k_stacked, after(b, 16 * 6, 0))
                    apart(sp)
                sp.wait_ge(lo_done, after(b, 6, 4))
                sp.dma_start(KD.rearrange("a p n -> p a n"), KS[:, :, 0:N0]).then_inc(k_parked, 16)
                sp.wait_ge(k_parked, after(b, 16, 16))
                if not first:
                    park_q(b, first)
                for r, part in enumerate(PART_K):
                    sp.dma_start(KX[D0 * r:D0 * r + D0, :, :], KD[part].rearrange("(g d) n -> d g n", g=G0)
                                 ).then_inc(k_stacked, 16)
                if first:
                    park_q(b, first)
                sp.wait_ge(q_parked, after(b, 16, 16))
                for r, part in enumerate(PART_Q):
                    sp.dma_start(QX[D0 * r:D0 * r + D0, :, :], QD[part].rearrange("(g d) n -> d g n", g=G0)
                                 ).then_inc(q_stacked, 16)

            stack(0, True)
            sp.dma_start(Xb[:, QT:TILES, :], xb[:, QT:TILES, :]).then_inc(loaded_rest, 16)
            for j in range(J):
                for r in range(2):
                    row = (2 * j + r) * D0
                    sp.dma_start(WoX[row:row + D0, :, :],
                                 wo0.rearrange("(k r j d) n -> j r d k n", r=2, j=J, d=D0)[j, r]
                                 ).then_inc(loaded_rest, 16)
            for dst, src in ((Wd, dense), (LA, loraA), (SA, sharedA)):
                sp.dma_start(dst[:], src.rearrange("(c p) n -> p c n", p=P)).then_inc(loaded_rest, 16)
            sp.dma_start(LB[:], loraB.rearrange("(c p) n -> p c n", p=P)).then_inc(loaded_rest, 16)
            sp.dma_start(SB[:], sharedB).then_inc(loaded_rest, 16)
            sp.dma_start(biasr[:], bias).then_inc(loaded_rest, 16)
            sp.dma_start(gcol[:], gate_rep).then_inc(loaded_rest, 16)

            def max_rows(b):
                for g in range(G0):
                    sp.wait_ge(nmt_split, after(b, 2 * G0, 2 * g + 2))
                    for s in range(2):
                        sp.dma_start(QX[R0 + s:R0 + s + 1, g, :].rearrange("o (c q) -> o c q", q=P),
                                     NMT[:, s, :]).then_inc(m_rows, 16)

            with sp.Fori(0, B - 1) as b:
                max_rows(b)
                stack(b + 1, False)
            max_rows(B - 1)

            if "B" in phases:
                sp.wait_ge(x_done, XB)
                sp.dma_start(Wv1[:], wv1.rearrange("(c p) n -> p c n", p=P)).then_inc(loaded_v1, 16)
                sp.dma_start(Wk1[:], wk1.rearrange("(c p) n -> p c n", p=P)).then_inc(loaded_k1, 16)
                sp.dma_start(Wq1[:], wq1.rearrange("(c p) n -> p c n", p=P)).then_inc(loaded_q1, 16)
                sp.dma_start(WR[:, :, 0:P], expertA.rearrange("(c p) n -> p c n", p=P)).then_inc(loaded_b2, 16)
                sp.dma_start(WR[:, :, P:P + E1], routeT.rearrange("(c p) n -> p c n", p=P)).then_inc(loaded_b2, 16)
                sp.dma_start(WB[:], expertB).then_inc(loaded_b2, 16)
                with sp.Fori(0, B) as b:
                    for g in range(G1):
                        sp.wait_ge(nmt_split, after(b, 2 * G1, 2 * g + 2, 2 * G0 * B))
                        for s in range(2):
                            sp.dma_start(Q1H[D1 + s:D1 + s + 1, g % 2, :].bitcast(F32).rearrange("o (c q) -> o c q", q=P),
                                         NMT1[:, s, :].bitcast(F32)).then_inc(m_rows, 16)
                    for qt in range(QT):
                        sp.wait_ge(x_done, after(b, 2, qt + 1, XB))
                        sp.dma_start(out[bass.ds(b * Q + qt * P, P), :], xt(b, qt)).then_inc(stored, 16)
                sp.wait_ge(stored, 16 * QT * B)
            else:
                sp.wait_ge(x_done, XB)
                sp.dma_start(out.rearrange("(t p) d -> p t d", p=P),
                             X[:].rearrange("p (t d) -> p t d", d=D)).then_inc(stored, 16)
                sp.wait_ge(stored, 16)

        @block.gpsimd
        def _(pool):
            def eye(tile, pattern, base, n):
                pool.wait_ge(consts, n)
                return nc.gpsimd.affine_select(out=tile, in_=tile, compare_op=ALU.not_equal, fill=1.0,
                                               base=base, pattern=pattern, channel_multiplier=1)

            def load_ctx(b):
                apart(pool)
                pool.dma_start(C[:], ctxT[bass.ds(b, 1), :, :].rearrange("o (c p) n -> p (o c) n", p=P)
                               ).then_inc(ctx_loaded, 16)

            nc.gpsimd.memset(ident[:], 0.0).then_inc(consts, 1)
            eye(ident[:], [[-1, P]], 0, 1).then_inc(consts, 1)
            nc.gpsimd.memset(identb[:], 0.0).then_inc(consts, 1)
            nc.gpsimd.memset(selA[:], 0.0).then_inc(consts, 1)
            nc.gpsimd.memset(eye32[:], 0.0).then_inc(consts, 1)
            nc.gpsimd.memset(halves[:, 0:1], 0.0).then_inc(consts, 1)
            pairs = VX[:].rearrange("p t (k r) c -> p t k (r c)", r=2)
            nc.gpsimd.memset(pairs[:, :, :, D0:3 * D0], 1.0).then_inc(consts, 1)
            pool.wait_ge(consts, 7)
            nc.gpsimd.memset(KX[R0:R0 + 2, :, :], 1.0).then_inc(consts, 1)
            pool.wait_ge(consts, 8)
            nc.gpsimd.memset(onesr[:], 1.0).then_inc(consts, 1)
            eye(identb[:], [[-1, P]], 0, 3).then_inc(consts, 1)
            eye(selA[:, 0, :].rearrange("p (j i) -> p j i", i=32), [[-32, 4], [0, 32]], -D0, 4).then_inc(consts, 1)
            for n in range(4):
                eye(eye32[:], [[0, 4], [-1, RANK]], -RANK * n, 11 + n).then_inc(consts, 1)
            eye(selA[:, 1, :].rearrange("p (j i) -> p j i", i=32), [[-32, 4], [0, 32]], 0, 4).then_inc(consts, 1)
            nc.gpsimd.memset(halves[:, 1:2], 1.0).then_inc(consts, 1)
            for j in range(J):
                for r in range(2):
                    pool.wait_ge(consts, 17 + 2 * j + r)
                    nc.gpsimd.memset(halves[32 * j:32 * j + D0, r:r + 1], 1.0 - r).then_inc(consts, 1)

            with pool.Fori(1, B) as b:
                pool.wait_ge(pv_done, after(b, NP0, 1 - NP0))
                load_ctx(b)

            if "B" in phases:
                pool.wait_ge(pv_done, NP0 * (B - 1) + 1)
                load_ctx(0)
                pool.wait_ge(x_done, XB)
                nc.gpsimd.memset(V1[:, :, :, D1:D1 + 1], 1.0).then_inc(consts_b, 1)
                pool.wait_ge(consts_b, 1)
                nc.gpsimd.memset(K1H[D1:D1 + 2, :, :].bitcast(F32), 1.0).then_inc(consts_b, 1)
                pool.wait_ge(consts_b, 2)
                nc.gpsimd.memset(one1[:], 1.0).then_inc(consts_b, 1)
                pool.wait_ge(consts_b, 3)
                nc.gpsimd.iota(rank[:], pattern=[[-1, E1]], base=E1, channel_multiplier=0,
                               allow_small_or_imprecise_dtypes=True).then_inc(consts_b, 1)

                def load_wo(g):
                    apart(pool)
                    pool.dma_start(Wo1[:, g % 2, :, :],
                                   wo1[g * J * D1:(g + 1) * J * D1, :].rearrange("(j d) n -> d j n", d=D1)
                                   ).then_inc(wo_loaded[g % 2], 16)

                def load_outputs(b):
                    pool.wait_ge(x_done, after(b, 2, 0, XB))
                    load_wo(0)
                    load_wo(1)
                    for g in range(2, G1):
                        pool.wait_ge(item_ready, after(b, NI, where[("Y", g - 2, ROWS - 1)] + 1))
                        load_wo(g)

                with pool.Fori(0, B - 1) as b:
                    load_outputs(b)
                    pool.wait_ge(item_ready, after(b, NI, where[("K", G1 - 1, NC0)] + 1))
                    load_ctx(b + 1)
                load_outputs(B - 1)

        @block.tensor
        def _(te):
            def turn_xn(b, L, base, bank):
                te.wait_ge(xn_ready[L], after(b, 2, 2, base * 2))
                for c in range(KC):
                    for qt in range(QT):
                        at = (c % 2) * Q + qt * P
                        mm = te.transpose(PS[:, bank + c // 2, at:at + P], XN[:, qt, c * P:(c + 1) * P], ident[:])
                mm.then_inc(xnt_ready[L], 1)

            def make_k(b, c):
                s, w = CH0[c]
                for k in range(KC):
                    mm = te.matmul(PS[:, c, 0:w], Wk[:, k, :], C[:, k, s:s + w], start=(k == 0), stop=(k == KC - 1))
                mm.then_inc(prod_ready, 1)

            def make_q(b):
                te.wait_ge(xnt_copied[0], after(b, 2, 2))
                for h in range(2):
                    for j in range(2):
                        for k in range(KC):
                            mm = te.matmul(PS[:, 4 + h, j * Q:(j + 1) * Q], Wq[:, k, (2 * h + j) * P:(2 * h + j + 1) * P],
                                           XNT[:, k, :], start=(k == 0), stop=(k == KC - 1))
                    mm.then_inc(prod_ready, 1)

            def make_v(b, q4, half=None):
                nt = min(4, len(KT0) - 4 * q4)
                for i in (range(2 * nt) if half is None else (half,)):
                    if i == 0:
                        te.wait_ge(rest_done, after(b, 6, (1, 2, 6, 6)[q4]))
                    t = 4 * q4 + i // 2
                    s, w = KT0[t]
                    for k in range(KC // 2 * (i % 2), KC // 2 * (i % 2 + 1)):
                        mm = te.matmul(PS[0:w, V_BANK[q4], i // 2 * P:(i // 2 + 1) * P], C[:, k, s:s + w],
                                       Wv[:, k, :], start=(k == 0), stop=(k == KC - 1))
                    if i == 2 * nt - 1:
                        mm.then_inc(v_ready, 1)

            def tail(b, ffn, nxt):
                nb = b + 1 if ffn else b
                for kind, i, m in tail_plan(ffn, nxt):
                    if kind == "piece":
                        if m == 0:
                            te.wait_ge(consts, 25)
                            te.wait_ge(k_stacked, after(nb, 16 * 6, 16 * 6))
                            te.wait_ge(q_stacked, after(nb, 16 * 6, 16 * 6))
                            te.wait_ge(v_copied, after(nb, 4, 2))
                        score_piece(nb, m)
                    elif kind == "max":
                        turn_max(nb, 0)
                    elif kind == "values":
                        make_v(nb, i, m)
                    else:
                        o, rows = PS[:, 2 + i, :], slice(i * P, (i + 1) * P)
                        if m < KC:
                            mm = te.matmul(o, XNT[:, m, rows], Wd[:, m, :], start=(m == 0), stop=False)
                        elif m == KC:
                            mm = te.matmul(o, AXS[:, rows], SB[:], start=False, stop=False)
                        elif m == KC + 1:
                            mm = te.matmul(o, onesr[:], biasr[:], start=False, stop=False)
                        else:
                            if m == KC + 2:
                                te.wait_ge(ga_ready, after(b, 2, i + 1))
                            c = m - (KC + 2)
                            mm = te.matmul(o, GA[:, i, c, :], LB[:, c, :], start=False, stop=(c == 3))
                        if m == FFN_STEPS - 1:
                            mm.then_inc(y_ready, 1)

            def score_piece(b, n):
                g, i = divmod(n, NS)
                row, c = divmod(i, NC0)
                s, w = CH0[c]
                if i == 0 and g >= 1:
                    te.wait_ge(nmt_split, after(b, 2 * G0, 2 * g))
                if n >= 2:
                    te.wait_ge(max_done, after(b, G0 * NS, n - 1))
                te.matmul(PS[:, n % 2, 0:w], QX[0:R0, g, row * P:(row + 1) * P], KX[0:R0, g, s:s + w],
                          start=True, stop=True).then_inc(s_ready, 1)

            def turn_max(b, g):
                te.wait_ge(nm_ready, after(b, G0, g + 1))
                te.transpose(PS[0:ROWS, 0, 0:P], nm[:], ident[:]).then_inc(nmt_ready, 1)

            def scores_t(b, g, t, h):
                n = g * len(KT0) + t
                s, w = KT0[t]
                if n >= 2 and h == 0:
                    te.wait_ge(exp_done, after(b, G0 * len(KT0), n - 1))
                if t == 0 and h == 0:
                    te.wait_ge(m_rows, after(b, 32 * G0, 32 * (g + 1)))
                o = PS[0:w, 2 + 2 * (n % 2) + h, :]
                te.matmul(o, KX[:, g, s:s + w], QX[:, g, h * BANK:(h + 1) * BANK], start=True, stop=False)
                mm = te.matmul(o, identb[0:w, 0:w],
                               mT[0:w, t, :].unsqueeze(1).to_broadcast([w, 2, Q]), start=False, stop=True)
                if h == 1:
                    mm.then_inc(st_ready, 1)

            def values(b, g, t):
                n = g * len(KT0) + t
                s, w = KT0[t]
                te.wait_ge(exp_done, after(b, G0 * len(KT0), n + 1))
                if t == 0 and g >= 2:
                    te.wait_ge(rec_done, after(b, G0, g - 1))
                for j in range(J):
                    mm = te.matmul(PS[32 * j:32 * j + 32, 6 + g % 2, 0:Q], VX[0:w, t, g, :],
                                   PT[0:w, n % 2, j * Q:(j + 1) * Q], start=(t == 0), stop=(t == len(KT0) - 1))
                mm.then_inc(pv_done, 1)

            def denominators(b, g):
                te.wait_ge(o_copied, after(b, G0, g + 1))
                te.matmul(PS[:, 6 + g % 2, Q:2 * Q], selA[:, g % 2, :], OS[:, g % 2, :], start=True, stop=True
                          ).then_inc(den_ready, 1)

            def attend(b):
                te.wait_ge(x_done, after(b, 4, 0, 1))
                te.wait_ge(masks_made, 2)
                te.wait_ge(v_copied, after(b, 4, 4))
                scores_t(b, 0, 0, 0)
                scores_t(b, 0, 0, 1)
                for g in range(G0):
                    for t in range(len(KT0)):
                        due = a_pieces(g, t)
                        for h in range(4):
                            if h < len(due):
                                score_piece(b, due[h])
                            if h < 2 and g * len(KT0) + t + 1 < NP0:
                                scores_t(b, *divmod(g * len(KT0) + t + 1, len(KT0)), h)
                            if h == 2:
                                if t == MAX_STEP and g + 1 < G0:
                                    turn_max(b, g + 1)
                                values(b, g, t)
                        if g >= 1 and t == (MAX_STEP if g + 1 < G0 else 1):
                            denominators(b, g - 1)

            def finish(b, nxt):
                if nxt:
                    te.wait_ge(ctx_loaded, after(b, 16, 16))
                    te.wait_ge(nmt_split, after(b, 2 * G0, 2 * G0))
                    make_k(b + 1, 0)
                    te.wait_ge(max_done, after(b, G0 * NS, G0 * NS))
                    make_k(b + 1, 1)
                denominators(b, G0 - 1)
                if nxt:
                    turn_xn(b + 1, 0, 0, 4)
                    make_k(b + 1, 2)
                    make_k(b + 1, 3)
                te.wait_ge(loaded_rest, 16 * (8 + 2 * J))
                te.wait_ge(on_ready, after(b, G0, G0))
                for qt in range(QT):
                    for k in range(G0 // 2):
                        mm = te.matmul(PS[:, 6 + qt, :], ON[:, k, qt * P:(qt + 1) * P], WoX[:, k, :],
                                       start=(k == 0), stop=(k == G0 // 2 - 1))
                    mm.then_inc(y_ready, 1)
                if nxt:
                    make_q(b + 1)
                turn_xn(b, 1, 0, 6)
                if nxt:
                    make_v(b + 1, 0)
                    te.wait_ge(rest_done, after(b, 6, 6 + 4))
                te.wait_ge(xnt_copied[1], after(b, 2, 2))
                for c in range(4):
                    for k in range(KC):
                        mm = te.matmul(PS[:, 2 + c // 2, (c % 2) * Q:(c % 2 + 1) * Q], LA[:, k, c * P:(c + 1) * P],
                                       XNT[:, k, :], start=(k == 0), stop=(k == KC - 1))
                    if c % 2:
                        mm.then_inc(ax_ready, 1)
                for k in range(KC):
                    mm = te.matmul(PS[0:RANK, 6, 0:Q], SA[:, k, :], XNT[:, k, :], start=(k == 0), stop=(k == KC - 1))
                mm.then_inc(ax_ready, 1)
                if nxt:
                    make_v(b + 1, 1)
                te.wait_ge(rp_ready, after(b, 1, 1))
                te.wait_ge(ax_copied, after(b, 3, 3))
                for qt in range(QT):
                    for c in range(4):
                        mm = te.matmul(PS[:, 7 - qt, 0:P], RP[:, qt * 4 + c, :], AXA[:, c, qt * P:(qt + 1) * P],
                                       start=(c == 0), stop=(c == 3))
                    mm.then_inc(rep_ready, 1)
                tail(b, True, nxt)

            te.wait_ge(loaded_k, 16)
            for c in range(NC0):
                te.wait_ge(loaded_ctx[c], 16)
                make_k(0, c)
            te.wait_ge(loaded_v, 16)
            make_v(0, 0)
            te.wait_ge(consts, 2)
            turn_xn(0, 0, 0, 4)
            te.wait_ge(loaded_q, 16)
            make_q(0)
            make_v(0, 1)
            tail(0, False, True)
            with te.Fori(0, B - 1) as b:
                attend(b)
                finish(b, True)
            attend(B - 1)
            finish(B - 1, False)

            if "B" not in phases:
                return
            te.wait_ge(consts_b, 4)
            te.wait_ge(x_done, XB)
            te.wait_ge(loaded_v1, 16)

            def v_tile(b, n, part=None):
                t = V_ORDER[n]
                s, w = KT1[t]
                if n == 0:
                    te.wait_ge(ctx_loaded, after(b, 16, 16, 16 * (B - 1)))
                if n >= 4 and not part:
                    te.wait_ge(v1_copied, after(b, T1, n - 3))
                for k in range(KC) if part is None else (part,):
                    lhs = XNT[:, k, s:s + w] if s < Q else C[:, k, s - Q:s - Q + w]
                    mm = te.matmul(PS[0:w, v_bank(n), 0:G1 * D1], lhs, Wv1[:, k, :], start=(k == 0), stop=(k == KC - 1))
                if k == KC - 1:
                    mm.then_inc(v1_ready, 1)

            def batch1(b, last):
                for n in range(V_FINISH, V_FINISH + V_START):
                    v_tile(b, n)
                te.wait_ge(x_done, after(b, 2, 0, XB))
                turn_xn(b, 0, B, 6)

                def item(n):
                    kind, g, i = items[n]
                    if n >= 2:
                        te.wait_ge(item_done, after(b, NI, n - 1))
                    bank = n % 2
                    if kind == "K":
                        s, w = (0, Q) if i == 0 else (Q + CH0[i - 1][0], CH0[i - 1][1])
                        for k in range(KC):
                            rhs = XNT[:, k, :] if i == 0 else C[:, k, s - Q:s - Q + w]
                            mm = te.matmul(PS[0:D1, bank, 0:w], Wk1[:, k, g * D1:(g + 1) * D1], rhs,
                                           start=(k == 0), stop=(k == KC - 1))
                    elif kind == "Q":
                        for j in range(2):
                            h = g * J + 2 * i + j
                            for k in range(KC):
                                mm = te.matmul(PS[0:D1, bank, j * Q:(j + 1) * Q], Wq1[:, k, h * D1:(h + 1) * D1],
                                               XNT[:, k, :], start=(k == 0), stop=(k == KC - 1))
                    elif kind == "S":
                        row, c = divmod(i, NC0)
                        s, w = CH1[c]
                        if i == 0:
                            te.wait_ge(item_done, after(b, NI, n))
                        mm = te.matmul(PS[:, bank, 0:w], Q1H[0:D1, g % 2, row * P:(row + 1) * P],
                                       K1H[0:D1, g % 2, s:s + w], start=True, stop=True)
                    elif kind == "M":
                        te.wait_ge(nm_ready, after(b, G1, g + 1, G0 * B))
                        mm = te.transpose(PS[0:ROWS, bank, 0:P], nm[:], ident[:])
                    elif kind == "R":
                        te.wait_ge(o1_copied, after(b, G1, g + 1))
                        for i in range(ROWS):
                            mm = te.matmul(PS[:, bank, i:i + 1], OS1[D1:D1 + 1, i * P:(i + 1) * P], one1[D1:D1 + 1, :],
                                           start=True, stop=True)
                    else:
                        if i == 0:
                            te.wait_ge(wo_loaded[g % 2], after(b, 16 * G1 // 2, 16 * (g // 2 + 1)))
                        mm = te.matmul(PS[:, bank, :], OS1[0:D1, i * P:(i + 1) * P], Wo1[:, g % 2, i // QT, :],
                                       start=True, stop=True)
                    mm.then_inc(item_ready, 1)

                def scores_t1(g, t, h):
                    n = g * T1 + t
                    s, w = KT1[t]
                    if n >= 2 and h == 0:
                        te.wait_ge(exp1_done, after(b, NP1, n - 1))
                    if t == 0 and h == 0:
                        te.wait_ge(m_rows, after(b, 32 * G1, 32 * (g + 1), 32 * G0 * B))
                    o, cols = PS[0:w, 2 + 2 * (n % 2) + h, :], slice(h * BANK, (h + 1) * BANK)
                    te.matmul(o, K1H[:, g % 2, s:s + w], Q1H[:, g % 2, cols], start=True, stop=False)
                    te.matmul(o, K1H[0:D1, g % 2, s:s + w], Q1L[:, g % 2, cols], start=False, stop=False)
                    mm = te.matmul(o, K1L[:, g % 2, s:s + w], Q1H[0:D1, g % 2, cols], start=False, stop=True)
                    if h == 1:
                        mm.then_inc(st1_ready, 1)

                def values1(g, t, h):
                    n = g * T1 + t
                    s, w = KT1[t]
                    if h == 0:
                        te.wait_ge(exp1_done, after(b, NP1, n + 1))
                        if t == 0 and g >= 1:
                            te.wait_ge(o1_copied, after(b, G1, g))
                    mm = te.matmul(PS[0:D1 + 1, 6 + h, :], V1[0:w, t, g, :], PT[0:w, n % 2, h * BANK:(h + 1) * BANK],
                                   start=(t == 0), stop=(t == T1 - 1))
                    if h == 1:
                        mm.then_inc(pv1_done, 1)

                te.wait_ge(xnt_copied[0], after(b, 2, 2, B * 2))
                te.wait_ge(loaded_k1, 16)
                te.wait_ge(loaded_q1, 16)
                for n in range(where[("M", 0, 0)] + 1):
                    item(n)
                    if items[n][0] == "S" and items[n][2] in V_BESIDE:
                        v_tile(b, *V_BESIDE[items[n][2]])
                for n in range(*step_items(0, -1)):
                    item(n)
                te.wait_ge(v1_copied, after(b, T1, T1))
                scores_t1(0, 0, 0)
                scores_t1(0, 0, 1)
                for g in range(G1):
                    for t in range(T1):
                        due = list(range(*step_items(g, t)))
                        for h in range(4):
                            for n in due[h:h + 1] if h < 3 else due[3:]:
                                item(n)
                            if h < 2 and g * T1 + t + 1 < NP1:
                                scores_t1(*divmod(g * T1 + t + 1, T1), h)
                            if h >= 2:
                                values1(g, t, h - 2)
                vs = (lambda *ns: None) if last else (lambda *ns: [v_tile(b + 1, n) for n in ns])
                vs(0, 1)
                for n in range(window_end[G1 - 1], NI):
                    item(n)
                vs(2, 3)
                turn_xn(b, 1, B, 6)
                vs(4)
                te.wait_ge(xnt_copied[1], after(b, 2, 2, B * 2))
                te.wait_ge(loaded_b2, 48)
                for qt in range(QT):
                    for k in range(KC):
                        mm = te.matmul(PS[:, 6 + qt, 0:P + E1], XNT[:, k, qt * P:(qt + 1) * P], WR[:, k, :],
                                       start=(k == 0), stop=(k == KC - 1))
                    mm.then_inc(h_ready, 1)
                vs(5, 6)
                for qt in range(QT):
                    te.wait_ge(wh_ready, after(b, 2, QT))
                    mm = te.transpose(PS[:, 6, qt * P:(qt + 1) * P], WH[:, qt, :], ident[:])
                mm.then_inc(wht_ready, 1)
                te.wait_ge(wht_copied, after(b, 1, 1))
                for qt in range(QT):
                    te.matmul(PS[:, 7 - qt, :], WHT[:, qt * P:(qt + 1) * P], WB[:], start=True, stop=True
                              ).then_inc(y_ready, 1)

            for n in range(V_FINISH):
                v_tile(0, n)
            with te.Fori(0, B - 1) as b:
                batch1(b, False)
            batch1(B - 1, True)

        @block.scalar
        def _(ae):
            def root(b, L, base):
                ae.wait_ge(var_ready[L], after(b, 1, 1, base))
                ae.activation(std[:], vpe[:], ACT.Sqrt).then_inc(std_ready[L], 1)

            def copy_xnt(b, L, base, bank):
                ae.wait_ge(xnt_ready[L], after(b, 1, 1, base))
                for h in range(2):
                    ae.copy(XNT[:, 2 * h:2 * h + 2, :].rearrange("p c q -> p (c q)"), PS[:, bank + h, :]
                            ).then_inc(xnt_copied[L], 1)

            def split_hi(b, n):
                ae.wait_ge(prod_ready, after(b, 6, n + 1))
                w = CH0[n][1] if n < 4 else BANK
                ae.copy(split_part(n, 0), PS[:, n, 0:w]).then_inc(hi_done, 1)

            def split_mid(b, n):
                ae.wait_ge(rest_done, after(b, 6, n + 1))
                w = CH0[n][1] if n < 4 else BANK
                ae.copy(split_part(n, 1), RS[:, n % 2, 0:w]).then_inc(mid_done, 1)

            def copy_values(b, q4):
                ae.wait_ge(v_ready, after(b, 4, q4 + 1))
                nt = min(4, len(KT0) - 4 * q4)
                w = KT0[4 * q4][1]
                for t in range(nt):
                    to = VX[0:w, 4 * q4 + t, :, :].rearrange("p (k r) (h d) -> p k (r h) d", r=2, h=2)
                    cp = ae.copy(to[:, :, 0::3, :],
                                 PS[0:w, V_BANK[q4], t * P:(t + 1) * P].rearrange("p (k r d) -> p k r d", r=2, d=D0))
                cp.then_inc(v_copied, 1)

            def attend(b):
                for g in range(G0):
                    for t, (s, w) in enumerate(KT0):
                        n = g * len(KT0) + t
                        ae.wait_ge(st_ready, after(b, G0 * len(KT0), n + 1))
                        if n >= 2:
                            ae.wait_ge(pv_done, after(b, G0 * len(KT0), n - 1))
                        ae.activation(PT[0:w, n % 2, :], PS[0:w, 2 + 2 * (n % 2):4 + 2 * (n % 2), :].rearrange("p a n -> p (a n)"),
                                      ACT.Exp, scale=D0 ** -0.5).then_inc(exp_done, 1)
                        if t == 0 and g >= 1:
                            copy_out(b, g - 1)
                copy_out(b, G0 - 1)

            def finish(b, nxt):
                if nxt:
                    root(b + 1, 0, 0)
                    copy_xnt(b + 1, 0, 0, 4)
                    ae.wait_ge(y_ready, after(b, 4, 2))
                    split_hi(b + 1, 0)
                root(b, 1, 0)
                if nxt:
                    split_mid(b + 1, 0)
                    for n in range(1, NC0):
                        split_hi(b + 1, n)
                        split_mid(b + 1, n)
                copy_xnt(b, 1, 0, 6)
                if nxt:
                    for n in (4, 5):
                        split_hi(b + 1, n)
                        split_mid(b + 1, n)
                    copy_values(b + 1, 0)
                for h in range(2):
                    ae.wait_ge(ax_ready, after(b, 3, h + 1))
                    ae.copy(AXA[:, 2 * h:2 * h + 2, :].rearrange("p c q -> p (c q)"), PS[:, 2 + h, :]).then_inc(ax_copied, 1)
                ae.wait_ge(ax_ready, after(b, 3, 3))
                ae.copy(AXS[:], PS[0:RANK, 6, 0:Q]).then_inc(ax_copied, 1)
                if nxt:
                    for q4 in range(1, 4):
                        copy_values(b + 1, q4)

            for n in range(NC0):
                split_hi(0, n)
                split_mid(0, n)
            ae.wait_ge(consts, 7)
            copy_values(0, 0)
            root(0, 0, 0)
            copy_xnt(0, 0, 0, 4)
            for n in (4, 5):
                split_hi(0, n)
                split_mid(0, n)
            for q4 in range(1, 4):
                copy_values(0, q4)
            ae.wait_ge(loaded_gates, 32)
            ae.activation(tg[:], gates[:], ACT.Tanh).then_inc(tanh_done, 1)
            with ae.Fori(0, B - 1) as b:
                attend(b)
                finish(b, True)
            attend(B - 1)
            finish(B - 1, False)

            if "B" not in phases:
                return
            ae.wait_ge(x_done, XB)
            ae.wait_ge(consts_b, 1)

            def copy_v(b, *ns):
                for n in ns:
                    t = V_ORDER[n]
                    w = KT1[t][1]
                    ae.wait_ge(v1_ready, after(b, T1, n + 1))
                    ae.copy(V1[0:w, t, :, 0:D1], PS[0:w, v_bank(n), 0:G1 * D1].rearrange("p (g d) -> p g d", d=D1)
                            ).then_inc(v1_copied, 1)

            def batch1(b, last):
                def halves(start, end):
                    for n in range(start, end):
                        if items[n][0] in "KQ":
                            ae.wait_ge(item_ready, after(b, NI, n + 1))
                            dst, w = half_of(n, K1H, Q1H)
                            ae.copy(dst, PS[0:D1, n % 2, 0:w]).then_inc(item_hi, 1)

                copy_v(b, V_FINISH)
                ae.wait_ge(x_done, after(b, 2, 0, XB))
                root(b, 0, B)
                copy_v(b, *range(V_FINISH + 1, V_FINISH + V_START))
                copy_xnt(b, 0, B, 6)
                halves(0, where[("M", 0, 0)])
                copy_v(b, *range(V_FINISH + V_START, T1))
                halves(*step_items(0, -1))

                def exp1(n):
                    w = KT1[n % T1][1]
                    ae.wait_ge(st1_ready, after(b, NP1, n + 1))
                    if n >= 2:
                        ae.wait_ge(pv1_done, after(b, NP1, n - 1))
                    ae.activation(PT[0:w, n % 2, :], PS[0:w, 2 + 2 * (n % 2):4 + 2 * (n % 2), :].rearrange("p a n -> p (a n)"),
                                  ACT.Exp, scale=D1 ** -0.5).then_inc(exp1_done, 1)

                exp1(0)
                for g in range(G1):
                    for t in range(T1):
                        if t == 0 and g >= 1:
                            copy_out1(b, g - 1)
                        start, end = step_items(g, t)
                        halves(start, min(start + 2, end))
                        if g * T1 + t + 1 < NP1:
                            exp1(g * T1 + t + 1)
                        halves(start + 2, end)
                copy_out1(b, G1 - 1)
                vs = (lambda *ns: None) if last else (lambda *ns: copy_v(b + 1, *ns))
                vs(0, 1, 2)
                root(b, 1, B)
                vs(3)
                copy_xnt(b, 1, B, 6)
                vs(4, 5, 6)
                ae.wait_ge(wht_ready, after(b, 1, 1))
                ae.copy(WHT[:], PS[:, 6, 0:Q]).then_inc(wht_copied, 1)

            copy_v(0, *range(V_FINISH))
            with ae.Fori(0, B - 1) as b:
                batch1(b, False)
            batch1(B - 1, True)

        @block.vector
        def _(ve):
            def ln_variance(b, L, base):
                for qt in range(QT):
                    apart(ve)
                    ve.bn_stats(stats[:, qt, :], xt(b, qt)).then_inc(ln_step[L], 1)
                ve.wait_ge(ln_step[L], after(b, 5, 2, base * 5))
                for qt in range(QT):
                    apart(ve)
                    ve.bn_aggr(mv[:, qt, :], stats[:, qt, :]).then_inc(ln_step[L], 1)
                ve.wait_ge(ln_step[L], after(b, 5, 4, base * 5))
                ve.tensor_scalar(vpe[:], mv[:, :, 1], EPS, None, ALU.add).then_inc(var_ready[L], 1)

            def ln_apply(b, L, base):
                ve.wait_ge(std_ready[L], after(b, 1, 1, base))
                ve.reciprocal(rstd[:], std[:]).then_inc(ln_step[L], 1)
                ve.wait_ge(ln_step[L], after(b, 5, 5, base * 5))
                for qt in range(QT):
                    ve.tensor_scalar(XN[:, qt, :], xt(b, qt), mv[:, qt, 0:1], rstd[:, qt:qt + 1],
                                     ALU.subtract, ALU.mult).then_inc(xn_ready[L], 1)

            def layer_norm(b, L, base):
                ln_variance(b, L, base)
                ln_apply(b, L, base)

            def split_rest(b, n):
                ve.wait_ge(hi_done, after(b, 6, n + 1))
                if n >= 2:
                    ve.wait_ge(lo_done, after(b, 6, n - 1))
                w = CH0[n][1] if n < 4 else BANK
                ve.tensor_tensor(RS[:, n % 2, 0:w], PS[:, n, 0:w], split_part(n, 0),
                                 ALU.subtract).then_inc(rest_done, 1)

            def split_lo(b, n):
                ve.wait_ge(mid_done, after(b, 6, n + 1))
                w = CH0[n][1] if n < 4 else BANK
                ve.tensor_tensor(split_part(n, 2), RS[:, n % 2, 0:w], split_part(n, 1),
                                 ALU.subtract).then_inc(lo_done, 1)

            def tail(b, ffn, nxt):
                nb = b + 1 if ffn else b
                for kind, i, m in tail_plan(ffn, nxt):
                    if kind == "piece":
                        max_piece(nb, m)
                    elif kind == "ffn" and m == FFN_STEPS - 1:
                        ve.wait_ge(y_ready, after(b, 4, 2 + i + 1))
                        ve.scalar_tensor_tensor(xt(b, i), PS[:, 2 + i, :], tg[:, 2:3], xt(b, i), ALU.mult, ALU.add
                                                ).then_inc(x_done, 1)
                if nxt:
                    row_max(nb, 0, not ffn)

            def max_piece(b, n):
                g, i = divmod(n, NS)
                row, c = divmod(i, NC0)
                s, w = CH0[c]
                ve.wait_ge(s_ready, after(b, G0 * NS, n + 1))
                if n >= 2:
                    ve.wait_ge(max_done, after(b, G0 * NS, n - 1))
                apart(ve)
                ve.tensor_tensor_reduce(junk[:, n % 2, 0:w], PS[:, n % 2, 0:w], mq[:, row % QT, s:s + w], 1.0,
                                        MASKED, ALU.add, ALU.max, pm[:, row, c:c + 1]).then_inc(max_done, 1)

            def row_max(b, g, first=False):
                ve.wait_ge(max_done, after(b, G0 * NS, (g + 1) * NS))
                if g >= 1:
                    ve.wait_ge(nmt_ready, after(b, G0, g))
                ve.tensor_reduce(nm[:], pm[:], AX.X, ALU.max, negate=True).then_inc(nm_ready, 1)
                ve.wait_ge(nmt_ready, after(b, G0, g + 1))
                if not first:
                    ve.wait_ge(m_rows, after(b, 32 * G0, 32 * g))
                ve.tensor_copy(NMT[:, 0, :], PS[0:ROWS, 0, 0:P]).then_inc(nmt_split, 1)
                ve.wait_ge(nmt_split, after(b, 2 * G0, 2 * g + 1))
                ve.tensor_tensor(NMT[:, 1, :], PS[0:ROWS, 0, 0:P], NMT[:, 0, :], ALU.subtract).then_inc(nmt_split, 1)

            def normalise(b, g):
                ve.wait_ge(den_ready, after(b, G0, g + 1))
                if g >= 1:
                    ve.wait_ge(on_ready, after(b, G0, g))
                ve.reciprocal(RC[:], PS[:, 6 + g % 2, Q:2 * Q]).then_inc(rec_done, 1)
                ve.wait_ge(rec_done, after(b, G0, g + 1))
                if g % 2 == 0:
                    ve.scalar_tensor_tensor(ON[:, g // 2, :], OS[:, 0, :], halves[:, 0:1], RC[:], ALU.mult, ALU.mult
                                            ).then_inc(on_ready, 1)
                else:
                    ve.scalar_tensor_tensor(odd[:], OS[:, 1, :], halves[:, 1:2], RC[:], ALU.mult, ALU.mult
                                            ).then_inc(odd_ready, 1)
                    ve.wait_ge(odd_ready, after(b, G0 // 2, g // 2 + 1))
                    ve.tensor_tensor(ON[:, g // 2, :], ON[:, g // 2, :], odd[:], ALU.add).then_inc(on_ready, 1)

            def attend(b, nxt):
                for g in range(G0):
                    if g + 1 < G0:
                        for n in range((g + 1) * NS, (g + 2) * NS):
                            max_piece(b, n)
                        row_max(b, g + 1)
                    if g >= 1:
                        normalise(b, g - 1)
                if nxt:
                    layer_norm(b + 1, 0, 0)
                normalise(b, G0 - 1)

            def finish(b, nxt):
                for qt in range(QT):
                    ve.wait_ge(y_ready, after(b, 4, qt + 1))
                    ve.scalar_tensor_tensor(xt(b, qt), PS[:, 6 + qt, :], tg[:, 0:1], xt(b, qt), ALU.mult, ALU.add
                                            ).then_inc(x_done, 1)
                ve.wait_ge(x_done, after(b, 4, 2, 1))
                ln_variance(b, 1, 0)
                if nxt:
                    split_rest(b + 1, 0)
                    ve.wait_ge(xnt_ready[0], after(b, 1, 2))
                ln_apply(b, 1, 0)
                if nxt:
                    split_lo(b + 1, 0)
                    for n in range(1, 6):
                        split_rest(b + 1, n)
                        split_lo(b + 1, n)
                    ve.wait_ge(lo_done, after(b, 6, 12))
                ve.tensor_tensor(RP, eye32[:].rearrange("p r k -> p (r k)").unsqueeze(1).to_broadcast([P, QT * 4, P]),
                                 gcol[:, bass.ds(b * (QT * 4), QT * 4)].unsqueeze(2).to_broadcast([P, QT * 4, P]),
                                 ALU.mult).then_inc(rp_ready, 1)
                for qt in range(QT):
                    ve.wait_ge(rep_ready, after(b, 2, qt + 1))
                    ve.tensor_tensor(GA[:, qt, :, :], PS[:, 7 - qt, 0:P].unsqueeze(1).to_broadcast([P, 4, P]),
                                     gcol[:, bass.ds(b * (QT * 4) + qt * 4, 4)].unsqueeze(2).to_broadcast([P, 4, P]),
                                     ALU.mult).then_inc(ga_ready, 1)
                tail(b, True, nxt)

            ve.sem_inc(x_done, 1)
            for n in range(NC0):
                split_rest(0, n)
                split_lo(0, n)
            ve.wait_ge(loaded_x, 16)
            layer_norm(0, 0, 0)
            ve.wait_ge(loaded_mask, 48)
            ve.tensor_scalar(mq[:], m8, -MASKED, MASKED, ALU.mult, ALU.add).then_inc(masks_made, 1)
            full = N0 // P
            ve.tensor_scalar(mT[:, 0:full, :], mT8[:, 0:full, :], -MASKED, MASKED, ALU.mult, ALU.add)
            ve.tensor_scalar(mT[0:N0 - full * P, full, :], mT8[0:N0 - full * P, full, :], -MASKED, MASKED,
                             ALU.mult, ALU.add).then_inc(masks_made, 1)
            for n in (4, 5):
                split_rest(0, n)
                split_lo(0, n)
            ve.wait_ge(masks_made, 2)
            tail(0, False, True)
            ve.wait_ge(loaded_rest, 16 * (8 + 2 * J))
            ve.wait_ge(tanh_done, 1)
            ve.wait_ge(consts, 25)
            with ve.Fori(0, B - 1) as b:
                attend(b, True)
                finish(b, True)
            attend(B - 1, False)
            finish(B - 1, False)

            if "B" not in phases:
                return
            ve.wait_ge(consts_b, 4)
            with ve.Fori(0, B) as b:
                ve.wait_ge(x_done, after(b, 2, 0, XB))

                def item(n):
                    kind, g, i = items[n]
                    bank = n % 2
                    ve.wait_ge(item_ready, after(b, NI, n + 1))
                    if kind in "KQ":
                        ve.wait_ge(item_hi, after(b, NHI, hi_order[items[n]] + 1))
                        hi, w = half_of(n, K1H, Q1H)
                        ve.tensor_tensor(half_of(n, K1L, Q1L)[0], PS[0:D1, bank, 0:w], hi.bitcast(F32),
                                         ALU.subtract).then_inc(item_done, 1)
                    elif kind == "S":
                        row, c = divmod(i, NC0)
                        ve.tensor_reduce(pm[:, row, c:c + 1], PS[:, bank, 0:CH1[c][1]], AX.X, ALU.max).then_inc(item_done, 1)
                        if i == NS - 1:
                            ve.wait_ge(item_done, after(b, NI, n + 1))
                            if g >= 1:
                                ve.wait_ge(item_ready, after(b, NI, where[("M", g - 1, 0)] + 1))
                            ve.tensor_reduce(nm[:], pm[:], AX.X, ALU.max, negate=True).then_inc(nm_ready, 1)
                    elif kind == "M":
                        if g >= 1:
                            ve.wait_ge(m_rows, after(b, 32 * G1, 32 * g, 32 * G0 * B))
                        ve.tensor_copy(NMT1[:, 0, :], PS[0:ROWS, bank, 0:P]).then_inc(nmt_split, 1)
                        ve.wait_ge(nmt_split, after(b, 2 * G1, 2 * g + 1, 2 * G0 * B))
                        ve.tensor_tensor(NMT1[:, 1, :], PS[0:ROWS, bank, 0:P], NMT1[:, 0, :].bitcast(F32),
                                         ALU.subtract).then_inc(nmt_split, 1)
                        ve.wait_ge(nmt_split, after(b, 2 * G1, 2 * g + 2, 2 * G0 * B))
                        ve.sem_inc(item_done, 1)
                    elif kind == "R":
                        ve.reciprocal(RC1[:], PS[:, bank, 0:ROWS]).then_inc(rec1_done, 1)
                        ve.wait_ge(rec1_done, after(b, G1, g + 1))
                        ve.tensor_scalar(RG1[:], RC1[:], tg[:, 1:2], None, ALU.mult).then_inc(item_done, 1)
                    else:
                        ve.wait_ge(item_done, after(b, NI, n if i < QT else n - 1))
                        ve.scalar_tensor_tensor(xt(b, i % QT), PS[:, bank, :], RG1[:, i:i + 1], xt(b, i % QT),
                                                ALU.mult, ALU.add).then_inc(item_done, 1)

                layer_norm(b, 0, B)
                for n in range(NI):
                    item(n)
                ve.wait_ge(item_done, after(b, NI, NI))
                layer_norm(b, 1, B)
                R = lambda qt, k: ve.wait_ge(rt_step, after(b, 10, 5 * qt + k))
                for qt in range(QT):
                    h, lg = PS[:, 6 + qt, 0:P], PS[:, 6 + qt, P:P + E1]
                    ve.wait_ge(h_ready, after(b, 2, qt + 1))
                    ve.tensor_reduce(top[:, qt, 0:1], lg, AX.X, ALU.max).then_inc(rt_step, 1)
                    R(qt, 1)
                    ve.tensor_scalar(lgt[:, qt, 0, :], lg, top[:, qt, 0:1], None, ALU.is_equal).then_inc(rt_step, 1)
                    R(qt, 2)
                    ve.tensor_tensor(lgt[:, qt, 1, :], lgt[:, qt, 0, :], rank[:], ALU.mult).then_inc(rt_step, 1)
                    R(qt, 3)
                    ve.tensor_reduce(top[:, qt, 1:2], lgt[:, qt, 1, :], AX.X, ALU.max).then_inc(rt_step, 1)
                    R(qt, 4)
                    ve.tensor_scalar(lgt[:, qt, 2, :], rank[:], top[:, qt, 1:2], top[:, qt, 0:1], ALU.is_equal, ALU.mult
                                     ).then_inc(rt_step, 1)
                    R(qt, 5)
                    ve.tensor_tensor(WH[:, qt, :].rearrange("p (e r) -> p e r", e=E1), h.rearrange("p (e r) -> p e r", e=E1),
                                     lgt[:, qt, 2, :].unsqueeze(2).to_broadcast([P, E1, RK1]), ALU.mult).then_inc(wh_ready, 1)
                for qt in range(QT):
                    ve.wait_ge(y_ready, after(b, 2, qt + 1, 4 * B))
                    ve.scalar_tensor_tensor(xt(b, qt), PS[:, 7 - qt, :], tg[:, 3:4], xt(b, qt), ALU.mult, ALU.add
                                            ).then_inc(x_done, 1)
                

def lay_out(i):
    import numpy as np

    a = {k: np.asarray(v) for k, v in i.items()}
    c = np.ascontiguousarray
    D = a["x"].shape[-1]
    mask = a["mask_SxS2_bk0"]
    wq = a["L0_xattn_w_q"].reshape(8, 4, 16, D)
    r = a["L0_ffn_lora_A"].shape[1]
    return {
        "x": c(a["x"].reshape(-1, D)),
        "ctxT": c(a["ctx_4096"].transpose(0, 2, 1)),
        "mask": c(mask),
        "maskT": c(mask.T),
        "g_xattn": c(a["g_xattn"]),
        "g_ffn": c(a["g_ffn"]),
        "wq0": c(wq.transpose(3, 1, 0, 2).reshape(D, -1)),
        "wk0": c(a["L0_xattn_w_k"].T),
        "wv0": c(a["L0_xattn_w_v"].T),
        "wo0": c(a["L0_xattn_w_out"].T),
        "gate_rep": c(np.repeat(a["L0_ffn_gate"].T, r, axis=0).reshape(4, 128, -1).transpose(1, 2, 0).reshape(128, -1)),
        "dense": c(a["L0_ffn_kernel"]),
        "bias": c(a["L0_ffn_bias"].reshape(1, -1)),
        "loraA": c(a["L0_ffn_lora_A"].reshape(-1, D).T),
        "loraB": c(a["L0_ffn_lora_B"].transpose(0, 2, 1).reshape(-1, D)),
        "sharedA": c(a["L0_ffn_lora_A_shared"].T),
        "sharedB": c(a["L0_ffn_lora_B_shared"].T),
        "wq1": c(a["L1_xattn_Wq"].T),
        "wk1": c(a["L1_xattn_Wk"].T),
        "wv1": c(a["L1_xattn_Wv"].T),
        "wo1": c(a["L1_xattn_Wo"].T),
        "routeT": c(a["L1_ffn_route_w"].T),
        "expertA": c(a["L1_ffn_A"].reshape(-1, D).T),
        "expertB": c(a["L1_ffn_Bw"].transpose(0, 2, 1).reshape(-1, D)),
    }


def kernel(**inputs):
    import numpy as np
    import concourse.bacc as bacc
    from concourse.bass_utils import run_bass_kernel_spmd

    nc = bacc.Bacc("TRN2", target_bir_lowering=False, num_devices=1)
    arrays = {f"in_{k}": v for k, v in lay_out(inputs).items()}
    args = [nc.dram_tensor(k, v.shape, mybir.dt.from_np(v.dtype), kind="ExternalInput").ap()
            for k, v in arrays.items()]
    shape = np.asarray(inputs["x"]).shape
    out = nc.dram_tensor("out_x", (shape[0] * shape[1], shape[2]), F32, kind="ExternalOutput").ap()
    flamingo_kernel(nc, *args, out)
    r = run_bass_kernel_spmd(nc, [arrays], core_ids=[0])
    return r.results[0]["out_x"].reshape(shape)
```
